# Optimizing a Trainium2 kernel written in Bass

```python
import numpy as np
import jax
import jax.numpy as jnp

def _softmax(x, axis=-1):
    return jax.nn.softmax(x, axis=axis)

def _gelu(x):
    return jax.nn.gelu(x, approximate=True)

def _silu(x):
    return jax.nn.silu(x)

def _sigmoid(x):
    return jax.nn.sigmoid(x)

def _layernorm(x, axis=-1, eps=1e-05):
    m = jnp.mean(x, axis=axis, keepdims=True)
    v = jnp.var(x, axis=axis, keepdims=True)
    return (x - m) / jnp.sqrt(v + eps)

def _scatter_add(tgt, idx, src, axis=0):
    return tgt.at[idx].add(src)

def _segment_sum(src, seg, n):
    return jax.ops.segment_sum(src, seg, n)
kernel_name = 'mk_xattn_ffn_d2_seqx_r8_9ba844'

def setup_inputs(seed: int=0):
    np.random.seed(seed)
    _w = jnp.asarray

    def _rec_inputs():
        import jax
        import jax.numpy as jnp
        _rk = jax.random.key(seed)
        x = -0.0003929 + 0.9999 * jax.random.normal(jax.random.fold_in(_rk, 1), (16, 128, 128), jnp.float32)
        _lenS = 128 - jax.random.randint(jax.random.fold_in(_rk, 7), (16,), 0, max(1, 128 // 4) + 1, jnp.int32)
        _lenS2 = 128 - jax.random.randint(jax.random.fold_in(_rk, 8), (16,), 0, max(1, 128 // 4) + 1, jnp.int32)
        _ctx_768P = jax.random.normal(jax.random.fold_in(_rk, 11), (16, 16, 96), jnp.float32)
        _ctx_768c = jax.random.dirichlet(jax.random.fold_in(_rk, 511), 0.3 * jnp.ones((16,), jnp.float32), (16, 128))
        _ctx_768t = jnp.einsum('bsk,bkd->bsd', _ctx_768c, _ctx_768P)
        _ctx_768t = _ctx_768t * jax.lax.rsqrt(jnp.mean(jnp.square(_ctx_768t)) + 1e-12) * 0.953939
        ctx_768 = -7.36909e-05 + 0.999899 * (_ctx_768t + 0.3 * jax.random.normal(jax.random.fold_in(_rk, 611), (16, 128, 96), jnp.float32))
        return (x, ctx_768)
    x, ctx_768 = _rec_inputs()

    def _L0_xattn_setup():
        import jax, jax.numpy as jnp
        import numpy as np
        IMG_DIM, TXT_DIM, HID = (128, 96, 128)
        B, LQ, LK = (8, 256, 256)
        key = jax.random.key(seed)
        ks = jax.random.split(key, 8)
        s_img = 1.0 / np.sqrt(IMG_DIM)
        s_txt = 1.0 / np.sqrt(TXT_DIM)
        return {'image_features': jax.random.normal(ks[0], (B, LQ, IMG_DIM), jnp.float32), 'text_features': jax.random.normal(ks[1], (B, LK, TXT_DIM), jnp.float32), 'Wq': jax.random.uniform(ks[2], (IMG_DIM, HID), jnp.float32, -s_img, s_img), 'bq': jax.random.uniform(ks[3], (HID,), jnp.float32, -s_img, s_img), 'Wk': jax.random.uniform(ks[4], (TXT_DIM, HID), jnp.float32, -s_txt, s_txt), 'bk': jax.random.uniform(ks[5], (HID,), jnp.float32, -s_txt, s_txt), 'Wv': jax.random.uniform(ks[6], (TXT_DIM, HID), jnp.float32, -s_txt, s_txt), 'bv': jax.random.uniform(ks[7], (HID,), jnp.float32, -s_txt, s_txt)}
    _L0_xattn_all = _L0_xattn_setup()
    _L0_xattn_in = {k: v for k, v in _L0_xattn_all.items() if k in ('Wq', 'bq', 'Wk', 'bk', 'Wv', 'bv')}
    del _L0_xattn_all

    def _L0_ffn_setup():
        import jax, jax.numpy as jnp
        import numpy as np
        TOP_K = 2
        key = jax.random.key(seed)
        k1, k2, k3, k4 = jax.random.split(key, 4)
        B, T, D, F, E = (2, 128, 128, 256, 8)
        x = jax.random.normal(k1, (B, T, D), dtype=jnp.float32)
        Wg = jax.random.normal(k2, (D, E), dtype=jnp.float32) * 0.02
        W1 = jax.random.normal(k3, (E, D, F), dtype=jnp.float32) * 0.02
        W2 = jax.random.normal(k4, (E, F, D), dtype=jnp.float32) * 0.02
        return {'x': x, 'Wg': Wg, 'W1': W1, 'W2': W2}
    _L0_ffn_all = _L0_ffn_setup()
    _L0_ffn_in = {k: v for k, v in _L0_ffn_all.items() if k in ('Wg', 'W1', 'W2')}
    del _L0_ffn_all

    def _L1_xattn_setup():
        import jax, jax.numpy as jnp
        import numpy as np
        HEADS = 16
        DIM_HEAD = 64
        key = jax.random.key(seed)
        ks = jax.random.split(key, 8)
        B, S, D = (16, 512, 128)
        K, DE = (77, 96)
        inner = HEADS * DIM_HEAD
        hidden_states = jax.random.normal(ks[0], (B, S, D), dtype=jnp.float32)
        encoder_hidden_states = jax.random.normal(ks[1], (B, K, DE), dtype=jnp.float32)
        sc_q = 1.0 / np.sqrt(D)
        sc_kv = 1.0 / np.sqrt(DE)
        sc_o = 1.0 / np.sqrt(inner)
        Wq = jax.random.normal(ks[2], (D, inner), dtype=jnp.float32) * sc_q
        Wk = jax.random.normal(ks[3], (DE, inner), dtype=jnp.float32) * sc_kv
        Wv = jax.random.normal(ks[4], (DE, inner), dtype=jnp.float32) * sc_kv
        Wo = jax.random.normal(ks[5], (inner, D), dtype=jnp.float32) * sc_o
        bo = jax.random.normal(ks[6], (D,), dtype=jnp.float32) * 0.01
        return {'hidden_states': hidden_states, 'encoder_hidden_states': encoder_hidden_states, 'Wq': Wq, 'Wk': Wk, 'Wv': Wv, 'Wo': Wo, 'bo': bo}
    _L1_xattn_all = _L1_xattn_setup()
    _L1_xattn_in = {k: v for k, v in _L1_xattn_all.items() if k in ('Wq', 'Wk', 'Wv', 'Wo', 'bo')}
    del _L1_xattn_all

    def _L1_ffn_setup():
        import jax, jax.numpy as jnp
        import numpy as np
        B, S, H, F, E, K = (2, 256, 128, 512, 8, 2)

        def _init_w(key, shape, fan_in):
            return jax.random.normal(key, shape, jnp.float32) * fan_in ** (-0.5)

        def _ffn(x, wi, bi, wo, bo):
            return jax.nn.selu(x @ wi + bi) @ wo + bo
        key = jax.random.key(seed)
        ks = jax.random.split(key, 6)
        return {'x': jax.random.normal(ks[0], (B, S, H), jnp.float32), 'gate_wi': _init_w(ks[1], (H, F), H), 'gate_bi': jnp.zeros((F,), jnp.float32), 'gate_wo': _init_w(ks[2], (F, H), F), 'gate_bo': jnp.zeros((H,), jnp.float32), 'exp_wi': _init_w(ks[3], (E, H, F), H), 'exp_bi': jnp.zeros((E, F), jnp.float32), 'exp_wo': _init_w(ks[4], (E, F, H), F), 'exp_bo': jnp.zeros((E, H), jnp.float32)}
    _L1_ffn_all = _L1_ffn_setup()
    _L1_ffn_in = {k: v for k, v in _L1_ffn_all.items() if k in ('gate_wi', 'gate_bi', 'gate_wo', 'gate_bo', 'exp_wi', 'exp_bi', 'exp_wo', 'exp_bo')}
    del _L1_ffn_all
    return {'x': x, 'ctx_768': ctx_768, 'L0_xattn_Wq': _L0_xattn_in['Wq'], 'L0_xattn_bq': _L0_xattn_in['bq'], 'L0_xattn_Wk': _L0_xattn_in['Wk'], 'L0_xattn_bk': _L0_xattn_in['bk'], 'L0_xattn_Wv': _L0_xattn_in['Wv'], 'L0_xattn_bv': _L0_xattn_in['bv'], 'L0_ffn_Wg': _L0_ffn_in['Wg'], 'L0_ffn_W1': _L0_ffn_in['W1'], 'L0_ffn_W2': _L0_ffn_in['W2'], 'L1_xattn_Wq': _L1_xattn_in['Wq'], 'L1_xattn_Wk': _L1_xattn_in['Wk'], 'L1_xattn_Wv': _L1_xattn_in['Wv'], 'L1_xattn_Wo': _L1_xattn_in['Wo'], 'L1_xattn_bo': _L1_xattn_in['bo'], 'L1_ffn_gate_wi': _L1_ffn_in['gate_wi'], 'L1_ffn_gate_bi': _L1_ffn_in['gate_bi'], 'L1_ffn_gate_wo': _L1_ffn_in['gate_wo'], 'L1_ffn_gate_bo': _L1_ffn_in['gate_bo'], 'L1_ffn_exp_wi': _L1_ffn_in['exp_wi'], 'L1_ffn_exp_bi': _L1_ffn_in['exp_bi'], 'L1_ffn_exp_wo': _L1_ffn_in['exp_wo'], 'L1_ffn_exp_bo': _L1_ffn_in['exp_bo']}

def reference(x, ctx_768, L0_xattn_Wq, L0_xattn_bq, L0_xattn_Wk, L0_xattn_bk, L0_xattn_Wv, L0_xattn_bv, L0_ffn_Wg, L0_ffn_W1, L0_ffn_W2, L1_xattn_Wq, L1_xattn_Wk, L1_xattn_Wv, L1_xattn_Wo, L1_xattn_bo, L1_ffn_gate_wi, L1_ffn_gate_bi, L1_ffn_gate_wo, L1_ffn_gate_bo, L1_ffn_exp_wi, L1_ffn_exp_bi, L1_ffn_exp_wo, L1_ffn_exp_bo):
    import jax
    import jax.numpy as jnp

    def _L0_xattn_ref(image_features, text_features, Wq, bq, Wk, bk, Wv, bv):
        import jax, jax.numpy as jnp
        import numpy as np
        IMG_DIM, TXT_DIM, HID = (128, 96, 128)
        B, LQ, LK = (8, 256, 256)
        query = jnp.einsum('bqi,ih->bqh', image_features, Wq) + bq
        key = jnp.einsum('bkt,th->bkh', text_features, Wk) + bk
        value = jnp.einsum('bkt,th->bkh', text_features, Wv) + bv
        scale = 1.0 / jnp.sqrt(jnp.asarray(HID, query.dtype))
        scores = jnp.einsum('bqh,bkh->bqk', query, key) * scale
        weights = jax.nn.softmax(scores, axis=-1)
        attended = jnp.einsum('bqk,bkh->bqh', weights, value)
        return attended

    def _L0_ffn_ref(x, Wg, W1, W2):
        import jax, jax.numpy as jnp
        import numpy as np
        TOP_K = 2
        B, T, D = x.shape
        E = Wg.shape[-1]
        xt = x.reshape(B * T, D)
        logits = xt @ Wg
        probs = jax.nn.softmax(logits, axis=-1)
        topw, topi = jax.lax.top_k(probs, TOP_K)
        topw = topw / jnp.sum(topw, axis=-1, keepdims=True)
        combine = jnp.sum(jax.nn.one_hot(topi, E, dtype=xt.dtype) * topw[..., None], axis=1)
        h = jax.nn.relu(jnp.einsum('nd,edf->enf', xt, W1))
        y = jnp.einsum('enf,efd->end', h, W2)
        out = jnp.einsum('ne,end->nd', combine, y)
        return out.reshape(B, T, D)

    def _L1_xattn_ref(hidden_states, encoder_hidden_states, Wq, Wk, Wv, Wo, bo):
        import jax, jax.numpy as jnp
        import numpy as np
        HEADS = 16
        DIM_HEAD = 64
        B, S, D = hidden_states.shape
        K = encoder_hidden_states.shape[1]
        H, Dh = (HEADS, DIM_HEAD)
        scale = 1.0 / np.sqrt(Dh)
        q = hidden_states @ Wq
        k = encoder_hidden_states @ Wk
        v = encoder_hidden_states @ Wv
        q = q.reshape(B, S, H, Dh).transpose(0, 2, 1, 3)
        k = k.reshape(B, K, H, Dh).transpose(0, 2, 1, 3)
        v = v.reshape(B, K, H, Dh).transpose(0, 2, 1, 3)
        scores = jnp.einsum('bhsd,bhkd->bhsk', q, k) * scale
        probs = jax.nn.softmax(scores, axis=-1)
        out = jnp.einsum('bhsk,bhkd->bhsd', probs, v)
        out = out.transpose(0, 2, 1, 3).reshape(B, S, H * Dh)
        out = out @ Wo + bo
        return out

    def _L1_ffn_ref(x, gate_wi, gate_bi, gate_wo, gate_bo, exp_wi, exp_bi, exp_wo, exp_bo):
        import jax, jax.numpy as jnp
        import numpy as np
        B, S, H, F, E, K = (2, 256, 128, 512, 8, 2)

        def _init_w(key, shape, fan_in):
            return jax.random.normal(key, shape, jnp.float32) * fan_in ** (-0.5)

        def _ffn(x, wi, bi, wo, bo):
            return jax.nn.selu(x @ wi + bi) @ wo + bo
        Bb, Ss, Hh = x.shape
        xf = x.reshape(-1, Hh)
        gate_logits = _ffn(xf, gate_wi, gate_bi, gate_wo, gate_bo)
        topv, topi = jax.lax.top_k(gate_logits, K)
        topv = topv / jnp.sum(topv, axis=-1, keepdims=True)
        onehot = (topi[..., None] == jnp.arange(E)).astype(x.dtype)
        w = jnp.einsum('nk,nke->ne', topv, onehot)
        h = jax.nn.selu(jnp.einsum('nh,ehf->enf', xf, exp_wi) + exp_bi[:, None, :])
        out_e = jnp.einsum('enf,efh->enh', h, exp_wo) + exp_bo[:, None, :]
        out = jnp.einsum('enh,ne->nh', out_e, w)
        return out.reshape(Bb, Ss, Hh)
    x = x + _L0_xattn_ref(_layernorm(x, axis=-1), ctx_768, L0_xattn_Wq, L0_xattn_bq, L0_xattn_Wk, L0_xattn_bk, L0_xattn_Wv, L0_xattn_bv)
    x = x + _L0_ffn_ref(_layernorm(x, axis=-1), L0_ffn_Wg, L0_ffn_W1, L0_ffn_W2)
    x = x + _L1_xattn_ref(_layernorm(x, axis=-1), ctx_768, L1_xattn_Wq, L1_xattn_Wk, L1_xattn_Wv, L1_xattn_Wo, L1_xattn_bo)
    x = x + _L1_ffn_ref(_layernorm(x, axis=-1), L1_ffn_gate_wi, L1_ffn_gate_bi, L1_ffn_gate_wo, L1_ffn_gate_bo, L1_ffn_exp_wi, L1_ffn_exp_bi, L1_ffn_exp_wo, L1_ffn_exp_bo)
    return x

_drawn_inputs = setup_inputs


def setup_inputs(seed=0):
    import zlib

    import numpy as np

    out = dict(_drawn_inputs(seed))
    spreads = {'L1_ffn_gate_bi': (0.0, 0.1),
     'L1_ffn_gate_bo': (0.0, 0.1),
     'L1_ffn_exp_bi': (0.0, 0.665),
     'L1_ffn_exp_bo': (0.0, 0.686)}
    factors = {'L0_xattn_bq': 6.092, 'L0_xattn_bk': 8.0, 'L1_xattn_bo': 2.861}
    for name, (base, spread) in spreads.items():
        noise = np.random.default_rng([zlib.crc32(name.encode()), seed]).standard_normal(out[name].shape)
        drawn = base * np.exp(spread * noise) if base else spread * noise
        out[name] = jnp.asarray(drawn.astype(out[name].dtype))
    for name, factor in factors.items():
        out[name] = (out[name] * factor).astype(out[name].dtype)
    return out
```

```python
from contextlib import ExitStack

import concourse.bass as bass
from concourse import mybir

F32 = mybir.dt.float32
I32 = mybir.dt.int32
U32 = mybir.dt.uint32
ALU = mybir.AluOpType
ACT = mybir.ActivationFunctionType
AX = mybir.AxisListType

P = 128
B = 16
TD = 96
GT = 4
G = B // GT
N = GT * P
HEADS, DH = 16, 64
PAIRS = HEADS // 2
E8 = 8
F0 = 256 // P
F1 = 512 // P
EPS = 1e-5
SELU_SCALE = 1.0507009873554805
SELU_ALPHA = 1.6732632423543772
LN_ALPHA = 0.5147757231540873


def stretch(ap, axis, n):
    return ap.broadcast_to([n if k == axis else m for k, m in enumerate(ap.shape)])


def build(nc, x, ctxT, Wq0, bq0, Wk0, bk0, Wv0, bv0, Wg, W1, W2, Wq1, Wk1, Wv1, Wo1, bo1,
          gwi, gbi, gwo, gbo, ewi, ebi, ewo, ebo, out):
    with ExitStack() as stack:
        def sb(name, shape, dt=F32):
            return stack.enter_context(nc.sbuf_tensor(name, shape, dt))

        sems = {}

        def sem(name):
            if name not in sems:
                sems[name] = stack.enter_context(nc.semaphore(name))
            return sems[name]

        def wait(eng, name, n):
            if not isinstance(n, int) or n > 0:
                eng.wait_ge(sem(name), n)

        xs = sb("xs", [P, B, P])
        xn_all = sb("xn_all", [P, B, P])
        xT_all = sb("xT_all", [P, B, P])
        ctx_all = sb("ctx_all", [TD, B, P])
        wq0, wk0, wv0 = sb("wq0", [P, P]), sb("wk0", [TD, P]), sb("wv0", [TD, P])
        bq0c, bk0c, bv0r = sb("bq0c", [P, 1]), sb("bk0c", [P, 1]), sb("bv0r", [P, P])
        wg = sb("wg", [P, E8])
        w1, w2 = sb("w1", [P, E8, F0, P]), sb("w2", [P, E8, F0, P])
        wq1, wo1 = sb("wq1", [P, PAIRS, P]), sb("wo1", [P, PAIRS, P])
        wk1, wv1 = sb("wk1", [TD, PAIRS, P]), sb("wv1", [TD, PAIRS, P])
        bo1r = sb("bo1r", [P, P])
        gwis, gwos = sb("gwis", [P, F1, P]), sb("gwos", [P, F1, P])
        gbic, gbor = sb("gbic", [P, F1]), sb("gbor", [P, P])
        ewis, ewos = sb("ewis", [P, E8, F1, P]), sb("ewos", [P, E8, F1, P])
        ebic, ebos = sb("ebic", [P, E8, F1]), sb("ebos", [E8, P])

        ident = sb("ident", [P, P])
        iota = sb("iota", [P, P])
        before = sb("before", [P, P])
        ones = sb("ones", [P, P])
        lnalpha = sb("lnalpha", [P, 1])

        stats, mv = sb("stats", [P, GT, 6]), sb("mv", [P, GT, 2])
        var, rstd = sb("var", [P, GT]), sb("rstd", [P, GT])
        neghalf, carrier = sb("neghalf", [P, GT]), sb("carrier", [P, 1])
        xn = [sb(f"xn{i}", [P, P]) for i in range(2)]
        xT = [sb(f"xT{i}", [P, P]) for i in range(2)]
        ctxb = [sb(f"ctxb{i}", [TD, P]) for i in range(2)]
        qT = [sb(f"qT{i}", [P, PAIRS, P]) for i in range(2)]
        kT = [sb(f"kT{i}", [P, PAIRS, P]) for i in range(2)]
        v = [sb(f"v{i}", [P, HEADS, DH + 1]) for i in range(2)]
        vA = [sb(f"vA{i}", [P, GT, P]) for i in range(3)]
        shifted = [sb(f"shifted{i}", [P, GT, P]) for i in range(2)]
        prob = [sb(f"prob{i}", [P, GT, P]) for i in range(4)]
        probT = [sb(f"probT{i}", [P, GT, P]) for i in range(4)]
        smax = [sb(f"smax{i}", [P, GT]) for i in range(2)]
        ssum = [sb(f"ssum{i}", [P, GT]) for i in range(2)]
        heads = [sb(f"heads{i}", [P, HEADS, DH]) for i in range(2)]
        headsT = sb("headsT", [P, PAIRS, P])
        hid = [sb(f"hid{i}", [P, F0, N]) for i in range(2)]
        act_u = [sb(f"act_u{i}", [P, N]) for i in range(2)]
        act_e = [sb(f"act_e{i}", [P, N]) for i in range(2)]

        top = sb("top", [P, GT, 8])
        topi = sb("topi", [P, GT, 8], U32)
        topf = sb("topf", [P, GT, 8])
        rt1, rt2 = sb("rt1", [P, GT, 8]), sb("rt2", [P, GT, 8])
        rsc = sb("rsc", [P, GT])
        lg = sb("lg", [P, GT, E8])
        glog = sb("glog", [P, GT, P])
        w0 = sb("w0", [P, B, E8])
        w_e = sb("w_e", [P, B, E8])

        flag, pos = sb("flag", [P, B]), sb("pos", [P, B])
        rowsum, total = sb("rowsum", [P, 1]), sb("total", [P, 1])
        ranks = sb("ranks", [P, B])
        nchf, nchi = sb("nchf", [P, 1]), sb("nchi", [P, 1], I32)
        pick = xT_all
        pickT = sb("pickT", [P, B, P])
        xc = sb("xc", [P, P])
        wc, wcs, wcT = sb("wc", [P, E8]), sb("wcs", [P, E8]), sb("wcT", [E8, P])
        yacc = sb("yacc", [P, P])

        ps = [stack.enter_context(nc.psum_tensor(f"ps{i}", [P, GT, P], F32)) for i in range(8)]

        block = stack.enter_context(nc.Block())

        A_STEPS = [("p", 0), ("p", 1), ("s", 0), ("p", 2), ("s", 1), ("a", 0),
                   ("p", 3), ("s", 2), ("a", 1), ("s", 3), ("a", 2), ("a", 3)]

        LN_ORDER = [("A", 0), ("A", 1)]
        for step, g in A_STEPS:
            if step == "p" and g + 2 < G:
                LN_ORDER.append(("A", g + 2))
            elif step == "a" and g > 0:
                LN_ORDER.append(("B", g - 1))
        LN_ORDER.append(("B", G - 1))
        LN_INDEX = {key: n for n, key in enumerate(LN_ORDER)}

        def tile(t, reg, n=1):
            return reg[:, t:t + n, :] if isinstance(t, int) else reg[:, bass.ds(t, n), :]

        @block.sync
        def _(sp):
            def load(dst, src, name):
                sp.dma_start(dst, src).then_inc(sem(name), 16)

            xv = x.rearrange("b p d -> p b d")
            cv = ctxT.rearrange("d (b p) -> d b p", b=B)
            for g in range(G):
                load(xs[:, GT * g:GT * (g + 1), :], xv[:, GT * g:GT * (g + 1), :], f"x_in{g}")
                if g == 0:
                    load(wq0[:], Wq0, "a_in")
                    load(wk0[:], Wk0, "a_in")
                    load(wv0[:], Wv0, "a_in")
                    load(bq0c[:], bq0.rearrange("(p a) -> p a", a=1), "a_in")
                    load(bk0c[:], bk0.rearrange("(p a) -> p a", a=1), "a_in")
                    load(bv0r[:], stretch(bv0.rearrange("(a n) -> a n", a=1), 0, P), "a_in")
                    load(ctx_all[:], cv, "a_in")
            load(wg[:], Wg, "b_in")
            load(w1[:], W1.rearrange("p (e f n) -> p e f n", e=E8, f=F0), "b_in")
            load(w2[:], W2.rearrange("p (e f n) -> p e f n", e=E8, f=F0), "b_in")
            load(wq1[:], Wq1.rearrange("p (c n) -> p c n", c=PAIRS), "c_in")
            load(wk1[:], Wk1.rearrange("p (c n) -> p c n", c=PAIRS), "c_in")
            load(wv1[:], Wv1.rearrange("p (c n) -> p c n", c=PAIRS), "c_in")
            load(wo1[:], Wo1.rearrange("p (c n) -> p c n", c=PAIRS), "c_in")
            load(bo1r[:], stretch(bo1.rearrange("(a n) -> a n", a=1), 0, P), "c_in")
            load(gwis[:], gwi.rearrange("p (c n) -> p c n", c=F1), "d_in")
            load(gwos[:], gwo.rearrange("p (c n) -> p c n", c=F1), "d_in")
            load(gbic[:], gbi, "d_in")
            load(gbor[:], stretch(gbo.rearrange("(a n) -> a n", a=1), 0, P), "d_in")
            load(ewis[:], ewi.rearrange("p (e f n) -> p e f n", e=E8, f=F1), "e_in")
            load(ewos[:], ewo.rearrange("p (e f n) -> p e f n", e=E8, f=F1), "e_in")
            load(ebic[:], ebi.rearrange("p (e f) -> p e f", e=E8), "e_in")
            load(ebos[:], ebo, "e_in")
            for b in range(2):
                load(ctxb[b][:], cv[:, b, :], f"ctx_in{b}")
            with sp.Fori(0, B // 2 - 1) as i:
                for par in range(2):
                    sp.wait_ge(sem("C_v1"), 2 * i + par + 1)
                    load(ctxb[par][:], cv[:, bass.ds(2 * i + 2 + par, 1), :], f"ctx_in{par}")
            sp.wait_ge(sem("E_count"), 1)
            n_chunks = sp.value_load(nchi[0:1, 0:1], min_val=1, max_val=B)
            ov = out.rearrange("b p d -> p b d")
            for q in range(G):
                sp.wait_ge(sem("E_x"), G * n_chunks + q + 1)
                sp.dma_start(ov[:, GT * q:GT * (q + 1), :], xs[:, GT * q:GT * (q + 1), :]).then_inc(sem("stored"), 16)
            sp.wait_ge(sem("stored"), 16 * G)

        @block.gpsimd
        def _(pool):
            pool.memset(neghalf[:], -0.5).then_inc(sem("filled"), 1)
            pool.memset(var[:], 1.0).then_inc(sem("filled"), 1)
            pool.memset(ones[:], 1.0).then_inc(sem("const"), 1)
            pool.memset(ident[:], 0.0).then_inc(sem("const"), 1)
            pool.memset(lnalpha[:], LN_ALPHA).then_inc(sem("const"), 1)
            for i in range(2):
                pool.memset(v[i][:, :, DH:DH + 1], 1.0).then_inc(sem("const"), 1)
            pool.iota(iota[:], pattern=[[1, P]], base=0, channel_multiplier=0,
                      allow_small_or_imprecise_dtypes=True).then_inc(sem("const"), 1)
            pool.wait_ge(sem("const"), 6)
            pool.affine_select(out=ident[:], in_=ident[:], compare_op=ALU.not_equal, fill=1.0, base=0,
                               pattern=[[-1, P]], channel_multiplier=1).then_inc(sem("const"), 1)
            pool.affine_select(out=before[:], in_=ones[:], compare_op=ALU.is_gt, fill=0.0, base=0,
                               pattern=[[1, P]], channel_multiplier=-1).then_inc(sem("const"), 1)

            def power(index):
                pool.wait_ge(sem("ln_var"), index + 1)
                pool.tensor_tensor(rstd[:], var[:], neghalf[:], ALU.pow).then_inc(sem("ln_rstd"), 1)

            pool.wait_ge(sem("filled"), 2)
            with pool.Fori(0, 2 * G) as n:
                power(n)
            pool.wait_ge(sem("c_in"), 16 * 5)
            with pool.Fori(0, B) as b:
                power(2 * G + b)
                pool.wait_ge(sem("C_ln"), b + 1)
                pool.tensor_tensor(xs[:, bass.ds(b, 1), :], xs[:, bass.ds(b, 1), :], bo1r[:].unsqueeze(1), ALU.add)\
                    .then_inc(sem("C_biased"), 1)
            with pool.Fori(0, G) as g:
                power(2 * G + B + g)

        CONST = 8

        @block.tensor
        def _(pe):
            def mm(dst, lhsT, rhs, start=True, stop=True):
                return pe.matmul(dst, lhsT, rhs, start=start, stop=stop)

            for name, n in (("B_y", 2),):
                pe.sem_inc(sem(name), n)
            pe.wait_ge(sem("const"), CONST)
            pe.wait_ge(sem("a_in"), 16 * 7)
            for step, g in A_STEPS:
                s = g % 2
                if step == "p":
                    pe.wait_ge(sem("A_ln"), g + 1)
                    wait(pe, "A_xT", g)
                    for t in range(GT):
                        last = pe.transpose(ps[0][:, t, :], xn_all[:, GT * g + t, :], ident[:])
                    last.then_inc(sem("A_tr"), 1)
                    wait(pe, "A_k_out", g)
                    last = mm(ps[2][:], wk0[:], ctx_all[:, GT * g:GT * (g + 1), :])
                    last.then_inc(sem("A_k"), 1)
                    wait(pe, "A_v_out", g)
                    for t in range(GT):
                        last = mm(ps[3][:, t, :], ctx_all[:, GT * g + t, :], wv0[:])
                    last.then_inc(sem("A_v"), 1)
                    pe.wait_ge(sem("A_xT"), g + 1)
                    wait(pe, "A_q_out", g)
                    mm(ps[1][:], wq0[:], xT_all[:, GT * g:GT * (g + 1), :]).then_inc(sem("A_q"), 1)
                elif step == "s":
                    pe.wait_ge(sem("A_q_out"), g + 1)
                    pe.wait_ge(sem("A_k_out"), g + 1)
                    wait(pe, "A_shift", g)
                    for t in range(GT):
                        last = mm(ps[4][:, t, :], qT[s][:, t, :], kT[s][:, t, :])
                    last.then_inc(sem("A_s"), 1)
                else:
                    pe.wait_ge(sem("A_exp"), g + 1)
                    wait(pe, "A_pT", g)
                    for t in range(GT):
                        last = pe.transpose(ps[5][:, t, :], prob[s][:, t, :], ident[:])
                    last.then_inc(sem("A_ptr"), 1)
                    pe.wait_ge(sem("A_pT"), g + 1)
                    pe.wait_ge(sem("A_v_out"), g + 1)
                    wait(pe, "A_x", g)
                    for t in range(GT):
                        last = mm(ps[6][:, t, :], probT[s][:, t, :], vA[g % 3][:, t, :])
                    last.then_inc(sem("A_o"), 1)

            pe.wait_ge(sem("b_in"), 16 * 3)
            for g in range(G):
                pe.wait_ge(sem("B_ln"), g + 1)
                wait(pe, "B_xT", g - 1)
                for t in range(GT):
                    last = pe.transpose(ps[g % 2][:, t, :], xn_all[:, GT * g + t, :], ident[:])
                last.then_inc(sem("B_tr"), 1)
            for g in range(G):
                pe.wait_ge(sem("B_xT"), g + 1)
                wait(pe, "B_lg", g - 1)
                for t in range(GT):
                    last = mm(ps[2 + g % 2][:, t, 0:E8], xT_all[:, GT * g + t, :], wg[:])
                last.then_inc(sem("B_l"), 1)
            pe.wait_ge(sem("B_lg"), G)
            pe.wait_ge(sem("A_x"), G)

            with pe.Fori(0, G) as g:
                def hidden(e):
                    for f in range(F0):
                        bank = F0 * (e % 2) + f
                        who = "B_relu_act" if f == 0 else "B_relu_dve"
                        wait(pe, who, E8 * g + e + 1)
                        mm(ps[bank][:], w1[:, e, f, :], xT_all[:, bass.ds(GT * g, GT), :]).then_inc(sem(f"B_h{f}"), 1)

                def output(e):
                    pe.wait_ge(sem("B_relu_act"), 2 + E8 * g + e + 1)
                    pe.wait_ge(sem("B_relu_dve"), 2 + E8 * g + e + 1)
                    pe.wait_ge(sem("B_y_out"), E8 * g + e + 1)
                    for t in range(GT):
                        for f in range(F0):
                            last = mm(ps[4 + e % 2][:, t, :], hid[e % 2][:, f, P * t:P * t + P],
                                      w2[:, e, f, :], start=f == 0, stop=f == F0 - 1)
                    last.then_inc(sem("B_y"), 1)

                hidden(0)
                for e in range(1, E8):
                    hidden(e)
                    output(e - 1)
                output(E8 - 1)
            pe.wait_ge(sem("B_y_out"), 2 + E8 * G)

            def transposes_p(b, s, u):
                for a in range(2):
                    pe.wait_ge(sem(f"C_exp{u}{a}"), b + 1)
                    if u == 0:
                        pe.wait_ge(sem(f"C_pT1{a}"), b) if not isinstance(b, int) or b > 0 else None
                    else:
                        wait(pe, f"C_hT{a}", b)
                        wait(pe, f"C_pT0{a}", b + 1)
                    for h in range(GT):
                        last = pe.transpose(ps[4 + a][:, h, :], prob[2 * u + a][:, h, :], ident[:])
                    last.then_inc(sem(f"C_ptr{u}{a}"), 1)

            def attend(b, s, u):
                for a in range(2):
                    pe.wait_ge(sem(f"C_pT{u}{a}"), b + 1)
                    if a == 0 and u == 0:
                        pe.wait_ge(sem("C_v0_out"), b + 1)
                        pe.wait_ge(sem("C_v1_out"), b + 1)
                    wait(pe, f"C_hd{1 - u}{a}", b if u == 0 else b + 1)
                    for h in range(GT):
                        last = mm(ps[6 + a][:, h, 0:DH + 1], probT[2 * u + a][:, h, :],
                                  v[s][:, 2 * GT * u + 2 * h + a, :])
                    last.then_inc(sem(f"C_o{u}{a}"), 1)

            def scores(b, s, u):
                if u == 0:
                    for name in ("C_q0_out", "C_q1_out", "C_k0_out", "C_k1_out"):
                        pe.wait_ge(sem(name), b + 1)
                for a in range(2):
                    wait(pe, f"C_shift{1 - u}{a}", b if u == 0 else b + 1)
                for h in range(GT):
                    for a in range(2):
                        last = mm(ps[2 + a][:, h, :], qT[s][DH * a:DH * (a + 1), GT * u + h, :],
                                  kT[s][DH * a:DH * (a + 1), GT * u + h, :])
                last.then_inc(sem(f"C_s{u}"), 1)

            def transpose_x(b, s):
                pe.wait_ge(sem("C_ln"), b + 1)
                wait(pe, "C_v0_out", b)
                pe.transpose(ps[0][:, 0, :], xn[s][:], ident[:]).then_inc(sem("C_xtr"), 1)

            def project_q(b, s):
                pe.wait_ge(sem("C_xT"), b + 1)
                wait(pe, "C_v1_out", b)
                for c, bank in ((0, 1), (1, 0)):
                    for i in range(GT):
                        last = mm(ps[bank][:, i, :], wq1[:, GT * c + i, :], xT[s][:])
                    last.then_inc(sem(f"C_q{c}"), 1)

            def project_k(b, s, n_ctx):
                pe.wait_ge(sem(f"ctx_in{s}"), n_ctx)
                for c, bank in ((0, 1), (1, 0)):
                    pe.wait_ge(sem(f"C_q{c}_out"), b + 1)
                    for i in range(GT):
                        last = mm(ps[bank][:, i, :], wk1[:, GT * c + i, :], ctxb[s][:])
                    last.then_inc(sem(f"C_k{c}"), 1)

            def project_v(b, s, after_out):
                for c, bank in ((0, 0), (1, 1)):
                    if c == 0:
                        pe.wait_ge(sem("C_k1_out"), b + 1)
                    else:
                        wait(pe, "C_k0_out", b + 1)
                        wait(pe, "C_x", after_out)
                    mm(ps[bank][:], ctxb[s][:], wv1[:, GT * c:GT * (c + 1), :]).then_inc(sem(f"C_v{c}"), 1)

            def transpose_heads(b, s):
                for a in range(2):
                    for u in range(2):
                        pe.wait_ge(sem(f"C_hd{u}{a}"), b + 1)
                for a in range(2):
                    wait(pe, f"C_pT0{a}", b + 2 if not isinstance(b, int) or b < B - 1 else B)
                    wait(pe, f"C_pT1{a}", b + 1)
                    for i in range(GT):
                        c = GT * a + i
                        last = pe.transpose(ps[4 + a][:, i, :], heads[s][:, 2 * c:2 * c + 2, :], ident[:])
                    last.then_inc(sem(f"C_htr{a}"), 1)

            def project_out(b, has_next):
                pe.wait_ge(sem("C_hT0"), b + 1)
                pe.wait_ge(sem("C_hT1"), b + 1)
                if has_next:
                    pe.wait_ge(sem("C_k0_out"), b + 3)
                else:
                    pe.wait_ge(sem("C_v1_out"), B)
                    wait(pe, "C_x", b)
                for c in range(PAIRS):
                    last = mm(ps[1][:, 0, :], headsT[:, c, :], wo1[:, c, :], start=c == 0, stop=c == PAIRS - 1)
                last.then_inc(sem("C_out"), 1)

            def body(b, s, n_ctx, first=False, last=False):
                scores(b, s, 0)
                if not first:
                    transposes_p(b - 1, 1 - s, 1)
                if not last:
                    transpose_x(b + 1, 1 - s)
                if not first:
                    attend(b - 1, 1 - s, 1)
                if not last:
                    project_q(b + 1, 1 - s)
                transposes_p(b, s, 0)
                scores(b, s, 1)
                attend(b, s, 0)
                if not first:
                    transpose_heads(b - 1, 1 - s)
                if not last:
                    project_k(b + 1, 1 - s, n_ctx)
                if not first:
                    project_out(b - 1, not last)
                if not last:
                    project_v(b + 1, 1 - s, b)

            pe.wait_ge(sem("c_in"), 16 * 5)
            transpose_x(0, 0)
            project_q(0, 0)
            project_k(0, 0, 16)
            project_v(0, 0, 0)
            body(0, 0, 16, first=True)
            body(1, 1, 32)
            with pe.Fori(0, B // 2 - 2) as i:
                body(2 * i + 2, 0, 16 * i + 32)
                body(2 * i + 3, 1, 16 * i + 48)
            body(B - 2, 0, 16 * (B // 2))
            body(B - 1, 1, None, last=True)
            transposes_p(B - 1, 1, 1)
            attend(B - 1, 1, 1)
            transpose_heads(B - 1, 1)
            project_out(B - 1, False)

            pe.wait_ge(sem("d_in"), 16 * 4)
            for g in range(G):
                pe.wait_ge(sem("D_ln"), g + 1)
                wait(pe, "D_xT", g - 1)
                for t in range(GT):
                    last = pe.transpose(ps[2 + g % 2][:, t, :], xn_all[:, GT * g + t, :], ident[:])
                last.then_inc(sem("D_tr"), 1)
            pe.wait_ge(sem("D_xT"), G)
            with pe.Fori(0, G) as g:
                for f in range(F1):
                    pe.wait_ge(sem(f"D_exp{f}"), g + 1)
                    mm(ps[f][:], gwis[:, f, :], xT_all[:, bass.ds(GT * g, GT), :]).then_inc(sem(f"D_h{f}"), 1)
                pe.wait_ge(sem("D_selu"), 2 + F1 * (g + 1))
                pe.wait_ge(sem("D_glog"), g + 1)
                for t in range(GT):
                    for f in range(F1):
                        last = mm(ps[4][:, t, :], hid[f // F0][:, f % F0, P * t:P * t + P],
                                  gwos[:, f, :], start=f == 0, stop=f == F1 - 1)
                last.then_inc(sem("D_l"), 1)

            pe.wait_ge(sem("E_rowsum"), 1)
            mm(ps[5][:, 0, 0:1], before[:], rowsum[:])
            mm(ps[5][:, 1, 0:1], ones[:], rowsum[:]).then_inc(sem("E_ranked"), 1)
            pe.wait_ge(sem("e_in"), 16 * 4)
            pe.wait_ge(sem("E_count"), 1)
            n_chunks = pe.value_load(nchi[0:1, 0:1], min_val=1, max_val=B)
            with pe.Fori(0, n_chunks) as c:
                pe.wait_ge(sem("E_pick"), c + 1)
                pe.wait_ge(sem("E_xc"), c + 1)
                for t in range(B):
                    last = mm(ps[6][:, 0, :], xn_all[:, t, :], pick[:, t, :], start=t == 0, stop=t == B - 1)
                last.then_inc(sem("E_gx"), 1)
                pe.wait_ge(sem("E_wc"), c + 1)
                for t in range(B):
                    last = mm(ps[7][:, 0, 0:E8], pick[:, t, :], w_e[:, t, :], start=t == 0, stop=t == B - 1)
                last.then_inc(sem("E_gw"), 1)
                for q in range(G):
                    pe.wait_ge(sem("E_pickT"), G * c + q + 1)
                    pe.wait_ge(sem("E_x"), G * (c + 1))
                    for t in range(GT):
                        last = pe.transpose(ps[4 + q % 2][:, t, :], pick[:, GT * q + t, :], ident[:])
                    last.then_inc(sem("E_ptr"), 1)
                pe.wait_ge(sem("E_wc"), c + 2)
                pe.transpose(ps[7][0:E8, 1, :], wc[:], ident[:]).then_inc(sem("E_wtr"), 1)

                def hidden(e):
                    pe.wait_ge(sem("E_u"), E8 * c + e + 1)
                    for f in range(F1):
                        last = mm(ps[e % 2][:, f, :], ewis[:, e, f, :], xc[:])
                    last.then_inc(sem("E_h"), 1)

                def output(e):
                    pe.wait_ge(sem("E_hid"), E8 * c + e + 1)
                    pe.wait_ge(sem("E_y_out"), E8 * c + e + 1)
                    for f in range(F1):
                        last = mm(ps[2 + e % 2][:, 0, :], hid[e % 2][:, 0, P * f:P * f + P], ewos[:, e, f, :],
                                  start=f == 0, stop=f == F1 - 1)
                    last.then_inc(sem("E_y"), 1)

                pe.wait_ge(sem("E_xc"), c + 2)
                hidden(0)
                pe.wait_ge(sem("E_wcT"), c + 1)
                mm(ps[7][:, 2, :], wcT[:], ebos[:]).then_inc(sem("E_bias"), 1)
                for e in range(1, E8):
                    hidden(e)
                    output(e - 1)
                output(E8 - 1)
                pe.wait_ge(sem("E_y_out"), 2 + E8 * (c + 1))
                pe.wait_ge(sem("E_pickT"), 2 + G * (c + 1))
                for q in range(G):
                    pe.wait_ge(sem("E_x"), G * c + q + 3)
                    for t in range(GT):
                        last = mm(ps[4 + q % 2][:, t, :], pickT[:, GT * q + t, :], yacc[:])
                    last.then_inc(sem("E_back"), 1)

        @block.scalar
        def _(act):
            for name, n in (("B_relu_act", 2), ("D_exp0", 1), ("D_exp1", 1), ("D_exp2", 1), ("D_exp3", 1),
                            ("E_pickT", 2)):
                act.sem_inc(sem(name), n)
            act.wait_ge(sem("a_in"), 16 * 7)
            for step, g in A_STEPS:
                s = g % 2
                if step == "p":
                    act.wait_ge(sem("A_tr"), g + 1)
                    act.copy(xT_all[:, GT * g:GT * (g + 1), :], ps[0][:]).then_inc(sem("A_xT"), 1)
                    act.wait_ge(sem("A_k"), g + 1)
                    wait(act, "A_s", g - 1)
                    act.activation(kT[s][:, 0:GT, :], ps[2][:], ACT.Identity, bias=bk0c[:]).then_inc(sem("A_k_out"), 1)
                    act.wait_ge(sem("A_q"), g + 1)
                    act.activation(qT[s][:, 0:GT, :], ps[1][:], ACT.Identity, bias=bq0c[:]).then_inc(sem("A_q_out"), 1)
                elif step == "s":
                    act.wait_ge(sem("A_shift"), g + 1)
                    wait(act, "A_ptr", g - 1)
                    wait(act, "A_sum", g - 1)
                    act.activation(prob[s][:], shifted[s][:], ACT.Exp, scale=P ** -0.5).then_inc(sem("A_exp"), 1)
                else:
                    act.wait_ge(sem("A_ptr"), g + 1)
                    wait(act, "A_o", g - 1)
                    act.copy(probT[s][:], ps[5][:]).then_inc(sem("A_pT"), 1)

            for g in range(G):
                act.wait_ge(sem("B_tr"), g + 1)
                act.copy(xT_all[:, GT * g:GT * (g + 1), :], ps[g % 2][:]).then_inc(sem("B_xT"), 1)
            for g in range(G):
                act.wait_ge(sem("B_lshift"), g + 1)
                act.activation(lg[:], rt1[:], ACT.Exp).then_inc(sem("B_lexp"), 1)
            with act.Fori(0, G) as g:
                for e in range(E8):
                    act.wait_ge(sem("B_h0"), E8 * g + e + 1)
                    act.wait_ge(sem("B_y"), E8 * g + e + 1)
                    act.activation(hid[e % 2][:, 0, :], ps[F0 * (e % 2)][:].rearrange("p t n -> p (t n)"), ACT.Relu).then_inc(sem("B_relu_act"), 1)

            def copy_pT(b, u):
                for a in range(2):
                    act.wait_ge(sem(f"C_ptr{u}{a}"), b + 1)
                    wait(act, f"C_o{u}{a}", b)
                    act.copy(probT[2 * u + a][:], ps[4 + a][:]).then_inc(sem(f"C_pT{u}{a}"), 1)

            def exp(b, u):
                for a in range(2):
                    act.wait_ge(sem(f"C_shift{u}{a}"), b + 1)
                    wait(act, f"C_ptr{u}{a}", b)
                    act.activation(prob[2 * u + a][:], shifted[a][:], ACT.Exp, scale=DH ** -0.5)\
                        .then_inc(sem(f"C_exp{u}{a}"), 1)

            def copy_x(b, s):
                act.wait_ge(sem("C_xtr"), b + 1)
                wait(act, "C_q1", b - 1)
                act.copy(xT[s][:], ps[0][:, 0, :]).then_inc(sem("C_xT"), 1)

            def copy_q(b, s):
                for c, bank in ((0, 1), (1, 0)):
                    act.wait_ge(sem(f"C_q{c}"), b + 1)
                    wait(act, "C_s1", b - 1)
                    act.copy(qT[s][:, GT * c:GT * (c + 1), :], ps[bank][:]).then_inc(sem(f"C_q{c}_out"), 1)

            def copy_k(b, s):
                act.wait_ge(sem("C_k0"), b + 1)
                wait(act, "C_s1", b - 1)
                act.copy(kT[s][:, 0:GT, :], ps[1][:]).then_inc(sem("C_k0_out"), 1)

            def copy_v(b, s):
                act.wait_ge(sem("C_v0"), b + 1)
                wait(act, "C_o11", b - 1)
                act.copy(v[s][:, 0:8, 0:DH], ps[0][:].rearrange("p t (h d) -> p (t h) d", d=DH)).then_inc(sem("C_v0_out"), 1)

            def copy_heads(b):
                for a in range(2):
                    act.wait_ge(sem(f"C_htr{a}"), b + 1)
                    wait(act, "C_out", b)
                    act.copy(headsT[:, GT * a:GT * (a + 1), :], ps[4 + a][:]).then_inc(sem(f"C_hT{a}"), 1)

            def body(b, s, first=False, last=False):
                if not first:
                    copy_pT(b - 1, 1)
                if not last:
                    copy_x(b + 1, 1 - s)
                exp(b, 0)
                if not last:
                    copy_q(b + 1, 1 - s)
                copy_pT(b, 0)
                exp(b, 1)
                if not first:
                    copy_heads(b - 1)
                if not last:
                    copy_k(b + 1, 1 - s)
                    copy_v(b + 1, 1 - s)

            copy_x(0, 0)
            copy_q(0, 0)
            copy_k(0, 0)
            copy_v(0, 0)
            body(0, 0, first=True)
            body(1, 1)
            with act.Fori(0, B // 2 - 2) as i:
                body(2 * i + 2, 0)
                body(2 * i + 3, 1)
            body(B - 2, 0)
            body(B - 1, 1, last=True)
            copy_pT(B - 1, 1)
            copy_heads(B - 1)

            for g in range(G):
                act.wait_ge(sem("D_tr"), g + 1)
                act.copy(xT_all[:, GT * g:GT * (g + 1), :], ps[2 + g % 2][:]).then_inc(sem("D_xT"), 1)
            with act.Fori(0, G) as g:
                for f in range(F1):
                    act.wait_ge(sem(f"D_h{f}"), g + 1)
                    act.wait_ge(sem("D_selu"), F1 * g + f + 1)
                    act.activation(act_u[f % 2][:], ps[f][:].rearrange("p t n -> p (t n)"), ACT.Identity, bias=gbic[:, f:f + 1])\
                        .then_inc(sem("D_u"), 1)
                    act.wait_ge(sem("D_u"), F1 * g + f + 1)
                    act.activation(act_e[f % 2][:], act_u[f % 2][:], ACT.Exp, bias=lnalpha[:])\
                        .then_inc(sem(f"D_exp{f}"), 1)

            act.wait_ge(sem("E_count"), 1)
            n_chunks = act.value_load(nchi[0:1, 0:1], min_val=1, max_val=B)
            with act.Fori(0, n_chunks) as c:
                for q in range(G):
                    act.wait_ge(sem("E_ptr"), G * c + q + 1)
                    act.copy(pickT[:, GT * q:GT * (q + 1), :], ps[4 + q % 2][:]).then_inc(sem("E_pickT"), 1)
                for e in range(E8):
                    act.wait_ge(sem("E_u"), 2 + E8 * c + e + 1)
                    act.activation(act_e[e % 2][:], act_u[e % 2][:], ACT.Exp, bias=lnalpha[:]).then_inc(sem("E_e"), 1)

        @block.vector
        def _(dve):
            class Chain:
                def __init__(self):
                    self.base, self.n = 0, 0

                def link(self, instruction, carried=False):
                    self.n += 1
                    instruction.then_inc(sem("dve"), 1)
                    dve.wait_ge(sem("dve"), self.base + self.n)
                    if carried and not isinstance(self.base, int):
                        carry_wait()

                def loop(self, i, step):
                    self.before, self.start = (self.base, self.n), self.n
                    self.base = self.base + i * step
                    self.step = step

                def end(self, turns):
                    assert self.n - self.start == self.step, self.n - self.start
                    self.base, self.n = self.before[0] + turns * self.step, self.before[1]

            chain = Chain()
            link = chain.link

            def carry_wait():
                dve.tensor_copy(carrier[:], neghalf[:, 0:1])

            def layer_norm(n, src, dst, done, index):
                for t in range(n):
                    last = dve.bn_stats(stats[:, t, :], src(t))
                link(last, carried=True)
                for t in range(n):
                    last = dve.bn_aggr(mv[:, t, :], stats[:, t, :])
                link(last)
                dve.tensor_scalar(var[:, 0:n], mv[:, 0:n, 1], EPS, None, ALU.add).then_inc(sem("ln_var"), 1)
                dve.wait_ge(sem("ln_rstd"), index + 1)
                for t in range(n):
                    last = dve.tensor_scalar(dst(t), src(t), mv[:, t, 0:1], rstd[:, t:t + 1], ALU.subtract, ALU.mult)
                last.then_inc(sem(done), 1)

            def norm_group(g, done, index):
                layer_norm(GT, lambda t: xs[:, GT * g + t, :], lambda t: xn_all[:, GT * g + t, :], done, index)

            def shift(bank, k, wait_free, done):
                link(dve.tensor_reduce(smax[k][:], ps[bank][:], AX.X, ALU.max))
                wait_free()
                dve.tensor_tensor(shifted[k][:], ps[bank][:], stretch(smax[k][:].unsqueeze(2), 2, P), ALU.subtract)\
                    .then_inc(sem(done), 1)

            def top2(values, dst):
                for t in range(GT):
                    last = dve.max(top[:, t, :], values(t))
                link(last, carried=True)
                for t in range(GT):
                    last = dve.max_index(topi[:, t, :], top[:, t, :], values(t))
                link(last)
                link(dve.tensor_copy(topf[:], topi[:]))
                link(dve.tensor_tensor(rsc[:].unsqueeze(2), top[:, :, 0:1], top[:, :, 1:2], ALU.add))
                link(dve.reciprocal(rsc[:], rsc[:]))
                link(dve.tensor_tensor(top[:, :, 0:2], top[:, :, 0:2], stretch(rsc[:].unsqueeze(2), 2, 2), ALU.mult))
                eight = stretch(iota[:, 0:E8].unsqueeze(1), 1, GT)
                for k, r in ((0, rt1), (1, rt2)):
                    link(dve.tensor_tensor(r[:], eight, stretch(topf[:, :, k:k + 1], 2, 8), ALU.is_equal))
                    link(dve.tensor_tensor(r[:], r[:], stretch(top[:, :, k:k + 1], 2, 8), ALU.mult))
                return dve.tensor_tensor(dst, rt1[:], rt2[:], ALU.add)

            for name, n in (("B_relu_dve", 2), ("B_y_out", 2), ("D_glog", 1), ("D_selu", 2),
                            ("E_xc", 1), ("E_wc", 1), ("E_u", 2), ("E_y_out", 2), ("E_x", G)):
                dve.sem_inc(sem(name), n)

            dve.wait_ge(sem("filled"), 2)

            def ln_a(g):
                dve.wait_ge(sem(f"x_in{g}"), 16)
                norm_group(g, "A_ln", LN_INDEX[("A", g)])

            ln_a(0)
            ln_a(1)
            dve.wait_ge(sem("a_in"), 16 * 7)
            for step, g in A_STEPS:
                s = g % 2
                if step == "p":
                    dve.wait_ge(sem("A_v"), g + 1)
                    wait(dve, "A_o", g - 2)
                    dve.tensor_tensor(vA[g % 3][:], ps[3][:], stretch(bv0r[:].unsqueeze(1), 1, GT), ALU.add)\
                        .then_inc(sem("A_v_out"), 1)
                    if g + 2 < G:
                        ln_a(g + 2)
                elif step == "s":
                    dve.wait_ge(sem("A_s"), g + 1)
                    shift(4, s, lambda: wait(dve, "A_exp", g - 1), "A_shift")
                else:
                    dve.wait_ge(sem("A_exp"), g + 1)
                    dve.tensor_reduce(ssum[0][:], prob[s][:], AX.X, ALU.add).then_inc(sem("A_sum"), 1)
                    dve.wait_ge(sem("A_sum"), g + 1)
                    link(dve.reciprocal(ssum[0][:], ssum[0][:]))
                    dve.wait_ge(sem("A_o"), g + 1)
                    for t in range(GT):
                        xt = xs[:, GT * g + t, :]
                        last = dve.scalar_tensor_tensor(xt, ps[6][:, t, :], ssum[0][:, t:t + 1], xt, ALU.mult, ALU.add)
                    last.then_inc(sem("A_x"), 1)
                    if g > 0:
                        dve.wait_ge(sem("A_x"), g)
                        norm_group(g - 1, "B_ln", LN_INDEX[("B", g - 1)])
            dve.wait_ge(sem("A_x"), G)
            norm_group(G - 1, "B_ln", LN_INDEX[("B", G - 1)])

            for g in range(G):
                dve.wait_ge(sem("B_l"), g + 1)
                bank = ps[2 + g % 2][:, :, 0:E8]
                link(dve.tensor_reduce(smax[0][:], bank, AX.X, ALU.max))
                dve.tensor_tensor(rt1[:], bank, stretch(smax[0][:].unsqueeze(2), 2, E8), ALU.subtract)\
                    .then_inc(sem("B_lshift"), 1)
                dve.wait_ge(sem("B_lexp"), g + 1)
                link(dve.tensor_reduce(rsc[:], lg[:], AX.X, ALU.add))
                link(dve.reciprocal(rsc[:], rsc[:]))
                link(dve.tensor_tensor(lg[:], lg[:], stretch(rsc[:].unsqueeze(2), 2, E8), ALU.mult))
                top2(lambda t: lg[:, t, :], w0[:, GT * g:GT * (g + 1), :]).then_inc(sem("B_lg"), 1)
            dve.wait_ge(sem("B_lg"), G)
            with dve.Fori(0, G) as g:
                def relu(e):
                    dve.wait_ge(sem("B_h1"), E8 * g + e + 1)
                    dve.wait_ge(sem("B_y"), E8 * g + e + 1)
                    dve.tensor_scalar(hid[e % 2][:, 1, :], ps[F0 * (e % 2) + 1][:].rearrange("p t n -> p (t n)"), 0.0, None, ALU.max)\
                        .then_inc(sem("B_relu_dve"), 1)

                def add(e):
                    dve.wait_ge(sem("B_y"), 2 + E8 * g + e + 1)
                    for t in range(GT):
                        xt = xs[:, bass.ds(GT * g + t, 1), :]
                        last = dve.scalar_tensor_tensor(xt, ps[4 + e % 2][:, t:t + 1, :],
                                                        w0[:, bass.ds(GT * g + t, 1), e], xt, ALU.mult, ALU.add)
                    last.then_inc(sem("B_y_out"), 1)
                    dve.wait_ge(sem("B_y_out"), 2 + E8 * g + e + 1)

                relu(0)
                for e in range(1, E8):
                    relu(e)
                    add(e - 1)
                add(E8 - 1)

            def ln_c(b, s):
                wait(dve, "C_xtr", b - 1)
                xt = xs[:, b, :] if isinstance(b, int) else xs[:, bass.ds(b, 1), :]
                layer_norm(1, lambda t: xt, lambda t: xn[s][:] if isinstance(b, int) else xn[s][:].unsqueeze(1), "C_ln", 2 * G + b)

            def shift_c(b, u):
                dve.wait_ge(sem(f"C_s{u}"), b + 1)
                for a in range(2):
                    shift(2 + a, a, lambda: wait(dve, f"C_exp{1 - u}{a}", b if u == 0 else b + 1), f"C_shift{u}{a}")

            def normalise(b, s, u):
                for a in range(2):
                    dve.wait_ge(sem(f"C_o{u}{a}"), b + 1)
                    bank = ps[6 + a]
                    link(dve.reciprocal(ssum[a][:].unsqueeze(2), bank[:, :, DH:DH + 1]))
                    if u == 0:
                        wait(dve, "C_htr1", b - 1)
                    dst = heads[s][:, 2 * GT * u:2 * GT * (u + 1), :].rearrange("p (i a) d -> p i a d", a=2)[:, :, a, :]
                    dve.tensor_tensor(dst, bank[:, :, 0:DH], stretch(ssum[a][:].unsqueeze(2), 2, DH), ALU.mult)\
                        .then_inc(sem(f"C_hd{u}{a}"), 1)

            def copy_k(b, s):
                dve.wait_ge(sem("C_k1"), b + 1)
                wait(dve, "C_s1", b - 1)
                dve.tensor_copy(kT[s][:, GT:2 * GT, :], ps[0][:]).then_inc(sem("C_k1_out"), 1)

            def copy_v(b, s):
                dve.wait_ge(sem("C_v1"), b + 1)
                wait(dve, "C_o11", b - 1)
                dve.tensor_copy(v[s][:, 8:16, 0:DH], ps[1][:].rearrange("p t (h d) -> p (t h) d", d=DH)).then_inc(sem("C_v1_out"), 1)

            def add_out(b):
                dve.wait_ge(sem("C_out"), b + 1)
                dve.wait_ge(sem("C_biased"), b + 1)
                xt = xs[:, b:b + 1, :] if isinstance(b, int) else xs[:, bass.ds(b, 1), :]
                dve.tensor_tensor(xt, ps[1][:, 0:1, :], xt, ALU.add).then_inc(sem("C_x"), 1)

            def body(b, s, first=False, last=False, norm=True):
                shift_c(b, 0)
                if not first:
                    normalise(b - 1, 1 - s, 1)
                shift_c(b, 1)
                normalise(b, s, 0)
                if not last:
                    copy_k(b + 1, 1 - s)
                if not first:
                    add_out(b - 1)
                if not last:
                    copy_v(b + 1, 1 - s)
                if norm:
                    ln_c(b + 2, s)

            dve.wait_ge(sem("const"), CONST)
            ln_c(0, 0)
            copy_k(0, 0)
            copy_v(0, 0)
            ln_c(1, 1)
            body(0, 0, first=True)
            body(1, 1)
            with dve.Fori(0, B // 2 - 2) as i:
                chain.loop(i, 2 * 10)
                body(2 * i + 2, 0)
                body(2 * i + 3, 1)
            chain.end(B // 2 - 2)
            body(B - 2, 0, norm=False)
            body(B - 1, 1, last=True, norm=False)
            normalise(B - 1, 1, 1)
            add_out(B - 1)

            dve.wait_ge(sem("C_x"), B)
            for g in range(G):
                norm_group(g, "D_ln", 2 * G + B + g)
            dve.wait_ge(sem("d_in"), 16 * 4)
            with dve.Fori(0, G) as g:
                chain.loop(g, 17)
                for f in range(F1):
                    dve.wait_ge(sem(f"D_exp{f}"), g + 2)
                    e, u = act_e[f % 2], act_u[f % 2]
                    link(dve.tensor_scalar(e[:], e[:], SELU_ALPHA, -SELU_ALPHA, ALU.min, ALU.add))
                    last = dve.scalar_tensor_tensor(hid[f // F0][:, f % F0, :], u[:], 0.0, e[:], ALU.max, ALU.add)
                    last.then_inc(sem("D_selu"), 1)
                dve.wait_ge(sem("D_l"), g + 1)
                dve.scalar_tensor_tensor(glog[:], ps[4][:], SELU_SCALE, stretch(gbor[:].unsqueeze(1), 1, GT), ALU.mult, ALU.add)\
                    .then_inc(sem("D_glog"), 1)
                dve.wait_ge(sem("D_glog"), g + 2)
                carry_wait()
                link(top2(lambda t: glog[:, t, :], w_e[:, bass.ds(GT * g, GT), :]))
                link(dve.tensor_scalar(rt1[:], w_e[:, bass.ds(GT * g, GT), :], 0.0, None, ALU.not_equal))
                link(dve.tensor_reduce(flag[:, bass.ds(GT * g, GT)], rt1[:], AX.X, ALU.max))
            chain.end(G)

            dve.tensor_reduce(rowsum[:], flag[:], AX.X, ALU.add).then_inc(sem("E_rowsum"), 1)
            link(dve.tensor_tensor_scan(ranks[:], ones[:, 0:B], flag[:], 0.0, ALU.mult, ALU.add))
            dve.wait_ge(sem("E_ranked"), 1)
            link(dve.tensor_scalar(ranks[:], ranks[:], ps[5][:, 0, 0:1], None, ALU.add))
            link(dve.tensor_tensor(pos[:], ranks[:], flag[:], ALU.mult))
            link(dve.tensor_scalar(pos[:], pos[:], -1.0, None, ALU.add))
            link(dve.tensor_copy(total[:], ps[5][:, 1, 0:1]))
            link(dve.tensor_scalar(ranks[:], iota[:, 0:B], float(P), total[:], ALU.mult, ALU.is_lt))
            link(dve.tensor_reduce(nchf[:], ranks[:], AX.X, ALU.add))
            link(dve.tensor_scalar(nchf[:], nchf[:], 1.0, None, ALU.max))
            dve.tensor_copy(nchi[:], nchf[:]).then_inc(sem("E_count"), 1)
            dve.wait_ge(sem("E_count"), 1)
            n_chunks = dve.value_load(nchi[0:1, 0:1], min_val=1, max_val=B)
            dve.wait_ge(sem("e_in"), 16 * 4)
            with dve.Fori(0, n_chunks) as c:
                chain.loop(c, 3 + E8)
                dve.tensor_tensor(pick[:], stretch(iota[:].unsqueeze(1), 1, B), stretch(pos[:].unsqueeze(2), 2, P), ALU.is_equal)\
                    .then_inc(sem("E_pick"), 1)
                dve.wait_ge(sem("E_gx"), c + 1)
                link(dve.tensor_scalar(pos[:], pos[:], -float(P), None, ALU.add))
                dve.tensor_copy(xc[:], ps[6][:, 0, :]).then_inc(sem("E_xc"), 1)
                dve.wait_ge(sem("E_gw"), c + 1)
                dve.tensor_copy(wc[:], ps[7][:, 0, 0:E8]).then_inc(sem("E_wc"), 1)
                dve.wait_ge(sem("E_wc"), c + 2)
                link(dve.tensor_scalar(wcs[:], wc[:], SELU_SCALE, None, ALU.mult))
                dve.wait_ge(sem("E_wtr"), c + 1)
                dve.tensor_copy(wcT[:], ps[7][0:E8, 1, :]).then_inc(sem("E_wcT"), 1)
                dve.wait_ge(sem("E_bias"), c + 1)
                link(dve.tensor_copy(yacc[:], ps[7][:, 2, :]))

                def add_bias(e):
                    dve.wait_ge(sem("E_h"), E8 * c + e + 1)
                    dve.tensor_tensor(act_u[e % 2][:].rearrange("p (f n) -> p f n", f=F1), ps[e % 2][:],
                                      stretch(ebic[:, e, :].unsqueeze(2), 2, P), ALU.add).then_inc(sem("E_u"), 1)

                def selu(e):
                    dve.wait_ge(sem("E_e"), E8 * c + e + 1)
                    ee, u = act_e[e % 2], act_u[e % 2]
                    link(dve.tensor_scalar(ee[:], ee[:], SELU_ALPHA, -SELU_ALPHA, ALU.min, ALU.add))
                    dve.scalar_tensor_tensor(hid[e % 2][:, 0, :], u[:], 0.0, ee[:], ALU.max, ALU.add)\
                        .then_inc(sem("E_hid"), 1)

                def add(e):
                    dve.wait_ge(sem("E_y"), E8 * c + e + 1)
                    last = dve.scalar_tensor_tensor(yacc[:], ps[2 + e % 2][:, 0, :], wcs[:, e:e + 1], yacc[:], ALU.mult, ALU.add)
                    last.then_inc(sem("E_y_out"), 1)
                    dve.wait_ge(sem("E_y_out"), 2 + E8 * c + e + 1)

                add_bias(0)
                for e in range(1, E8):
                    add_bias(e)
                    selu(e - 1)
                    if e >= 2:
                        add(e - 2)
                selu(E8 - 1)
                add(E8 - 2)
                add(E8 - 1)
                for q in range(G):
                    dve.wait_ge(sem("E_back"), G * c + q + 1)
                    xt = xs[:, GT * q:GT * (q + 1), :]
                    dve.tensor_tensor(xt, ps[4 + q % 2][:], xt, ALU.add).then_inc(sem("E_x"), 1)
            chain.end(0)


_OUT = (B, P, P)


def kernel(**inputs):
    import numpy as np
    import concourse.bacc as bacc
    from concourse.bass_utils import run_bass_kernel_spmd

    a = {k: np.asarray(w) for k, w in inputs.items()}
    laid = {
        "x": a["x"], "ctxT": a["ctx_768"].reshape(B * P, TD).T,
        "Wq0": a["L0_xattn_Wq"], "bq0": a["L0_xattn_bq"], "Wk0": a["L0_xattn_Wk"], "bk0": a["L0_xattn_bk"],
        "Wv0": a["L0_xattn_Wv"], "bv0": a["L0_xattn_bv"], "Wg": a["L0_ffn_Wg"],
        "W1": a["L0_ffn_W1"].transpose(1, 0, 2).reshape(P, -1),
        "W2": a["L0_ffn_W2"].reshape(E8, F0, P, P).transpose(2, 0, 1, 3).reshape(P, -1),
        "Wq1": a["L1_xattn_Wq"], "Wk1": a["L1_xattn_Wk"], "Wv1": a["L1_xattn_Wv"],
        "Wo1": a["L1_xattn_Wo"].reshape(PAIRS, P, P).transpose(1, 0, 2).reshape(P, -1), "bo1": a["L1_xattn_bo"],
        "gwi": a["L1_ffn_gate_wi"], "gbi": a["L1_ffn_gate_bi"].reshape(F1, P).T,
        "gwo": a["L1_ffn_gate_wo"].reshape(F1, P, P).transpose(1, 0, 2).reshape(P, -1), "gbo": a["L1_ffn_gate_bo"],
        "ewi": a["L1_ffn_exp_wi"].transpose(1, 0, 2).reshape(P, -1),
        "ebi": a["L1_ffn_exp_bi"].reshape(E8 * F1, P).T,
        "ewo": a["L1_ffn_exp_wo"].reshape(E8, F1, P, P).transpose(2, 0, 1, 3).reshape(P, -1),
        "ebo": a["L1_ffn_exp_bo"],
    }
    nc = bacc.Bacc("TRN2", target_bir_lowering=False, num_devices=1)
    arrays, args = {}, []
    for name, w in laid.items():
        w = np.ascontiguousarray(w)
        arrays[f"in_{name}"] = w
        args.append(nc.dram_tensor(f"in_{name}", w.shape, mybir.dt.from_np(w.dtype), kind="ExternalInput").ap())
    args.append(nc.dram_tensor("out_x", _OUT, F32, kind="ExternalOutput").ap())
    build(nc, *args)
    result = run_bass_kernel_spmd(nc, [arrays], core_ids=[0])
    return result.results[0]["out_x"]
```

```python
from contextlib import ExitStack

import concourse.bass as bass
from concourse import mybir

F32 = mybir.dt.float32
BF16 = mybir.dt.bfloat16
I32 = mybir.dt.int32
U32 = mybir.dt.uint32
ALU = mybir.AluOpType
ACT = mybir.ActivationFunctionType
AX = mybir.AxisListType

P = 128
B = 16
TD = 96
GT = 4
G = B // GT
N = GT * P
HEADS, DH = 16, 64
PAIRS = HEADS // 2
E8 = 8
F0 = 256 // P
F1 = 512 // P
EPS = 1e-5
SLOTS = 2 * P
SELU_SCALE = 1.0507009873554805
SELU_ALPHA = 1.6732632423543772
LN_ALPHA = 0.5147757231540873


def stretch(ap, axis, n):
    return ap.broadcast_to([n if k == axis else m for k, m in enumerate(ap.shape)])


def build(nc, x, ctxT, Wq0, bq0, Wk0, bk0, Wv0, bv0, Wg, W1, W2, Wq1, Wk1, Wv1, Wo1, bo1,
          gwi, gbi, gwo, gbo, ewi, ebi, ewo, ebo, out):
    with ExitStack() as stack:
        def sb(name, shape, dt=F32):
            return stack.enter_context(nc.sbuf_tensor(name, shape, dt))

        sems = {}

        def sem(name):
            if name not in sems:
                sems[name] = stack.enter_context(nc.semaphore(name))
            return sems[name]

        def wait(eng, name, n):
            if not isinstance(n, int) or n > 0:
                eng.wait_ge(sem(name), n)

        xs = sb("xs", [P, B, P])
        xT_all = sb("xT_all", [P, B, P])
        wq0, wk0, wv0 = sb("wq0", [P, P]), sb("wk0", [TD, P]), sb("wv0", [TD, P])
        bq0c, bk0c, bv0r = sb("bq0c", [P, 1]), sb("bk0c", [P, 1]), sb("bv0r", [P, P])
        wg = sb("wg", [P, E8])
        w12 = sb("w12", [P, 2, E8, F0, P])
        w1, w2 = w12[:, 0, :, :, :], w12[:, 1, :, :, :]
        xn3 = w12[:].rearrange("p a e f n -> p (a e f n)").bitcast(BF16)[:, 0:3 * B * P]\
            .rearrange("p (k t n) -> p k t n", k=3, t=B)
        wq1, wo1 = sb("wq1", [P, PAIRS, P]), sb("wo1", [P, PAIRS, P])
        wk1, wv1 = sb("wk1", [TD, PAIRS, P]), sb("wv1", [TD, PAIRS, P])
        bo1r = sb("bo1r", [P, P])
        gwis, gwos = sb("gwis", [P, F1, P]), sb("gwos", [P, F1, P])
        gbic, gbor = sb("gbic", [P, F1]), sb("gbor", [P, P])
        ewis, ewos = sb("ewis", [P, E8, F1, P]), sb("ewos", [P, E8, F1, P])
        ebic, ebos = sb("ebic", [P, E8, F1]), sb("ebos", [E8, P])

        ident = sb("ident", [P, P])
        iota = sb("iota", [P, P])
        before = sb("before", [P, P])
        ones = sb("ones", [P, P])
        lnalpha = sb("lnalpha", [P, 1])

        stats, mv = sb("stats", [P, GT, 6]), sb("mv", [P, GT, 2])
        var, rstd = sb("var", [P, GT]), sb("rstd", [P, GT])
        neghalf, carrier = sb("neghalf", [P, GT]), sb("carrier", [P, 1])
        carrier_p = sb("carrier_p", [P, 1])
        ctxg = sb("ctxg", [TD, GT, P])
        xng, xTg = sb("xng", [P, GT, P]), sb("xTg", [P, GT, P])
        vA = sb("vA", [P, GT, P])
        xn = [sb(f"xn{i}", [P, P]) for i in range(2)]
        xnD = [sb(f"xnD{i}", [P, P]) for i in range(2)]
        xT = [sb(f"xT{i}", [P, P]) for i in range(2)]
        ctxb = [sb(f"ctxb{i}", [TD, P]) for i in range(2)]
        qk = sb("qk", [P, 4, PAIRS, P])
        qT, kT = [qk[:, i, :, :] for i in range(2)], [qk[:, 2 + i, :, :] for i in range(2)]
        pick = qk[:].rearrange("p a c n -> p (a c n)").bitcast(BF16)[:, 0:B * SLOTS]\
            .rearrange("p (t s) -> p t s", t=B)
        v = [sb(f"v{i}", [P, HEADS, DH + 1]) for i in range(2)]
        shifted = [sb(f"shifted{i}", [P, GT, P]) for i in range(2)]
        pb = sb("pb", [P, 8, GT, P])
        prob, probT = [pb[:, i, :, :] for i in range(4)], [pb[:, 4 + i, :, :] for i in range(4)]
        pickT = pb[:].rearrange("p a c n -> p (a c n)").bitcast(BF16)[:, 0:B * SLOTS]\
            .rearrange("p (t h n) -> p t h n", t=B, h=2)
        smax = [sb(f"smax{i}", [P, GT]) for i in range(2)]
        ssum = [sb(f"ssum{i}", [P, GT]) for i in range(2)]
        heads = [sb(f"heads{i}", [P, HEADS, DH]) for i in range(2)]
        headsT = sb("headsT", [P, PAIRS, P])
        hid = [sb(f"hid{i}", [P, F1, SLOTS]) for i in range(2)]
        act_u = [sb(f"act_u{i}", [P, F1, SLOTS]) for i in range(2)]
        act_e = [sb(f"act_e{i}", [P, F1, SLOTS]) for i in range(2)]
        hidB = [[hid[k][:, F0 * f:F0 * (f + 1), :].rearrange("p a n -> p (a n)") for f in range(F0)] for k in range(2)]
        hidD = [[h[:, F0 * i:F0 * (i + 1), :].rearrange("p a n -> p (a n)") for h in hid for i in range(2)],
                [pb[:, i, :, :].rearrange("p a n -> p (a n)") for i in range(F1)]]

        top = sb("top", [P, GT, 8])
        topi = sb("topi", [P, GT, 8], U32)
        topf = sb("topf", [P, GT, 8])
        rt1, rt2 = sb("rt1", [P, GT, 8]), sb("rt2", [P, GT, 8])
        rsc = sb("rsc", [P, GT])
        lg = sb("lg", [P, GT, E8])
        glog = [sb(f"glog{i}", [P, GT, P]) for i in range(2)]
        w0 = sb("w0", [P, B, E8])
        w_e = sb("w_e", [P, B, E8])

        topv16, topi16 = sb("topv16", [P, B, 2]), sb("topi16", [P, B, 2])
        rt16 = sb("rt16", [P, 2, B, E8])
        flag, pos = sb("flag", [P, B]), sb("pos", [P, B])
        rowsum, total = sb("rowsum", [P, 1]), sb("total", [P, 1])
        ranks = sb("ranks", [P, B])
        nchf, nchi = sb("nchf", [P, 1]), sb("nchi", [P, 1], I32)
        w3 = sb("w3", [P, B, 3, E8], BF16)
        y3 = sb("y3", [P, 3, 2, P], BF16)
        iotab, identb = sb("iotab", [P, SLOTS], BF16), sb("identb", [P, P], BF16)
        xc = sb("xc", [P, SLOTS])
        wc3 = sb("wc3", [P, 2, 3, E8])
        wc, wcs, wcT = sb("wc", [P, 2, E8]), sb("wcs", [P, 2, E8]), sb("wcT", [E8, 2, P])
        yacc = sb("yacc", [P, 2, P])
        rest, rest_p = sb("rest", [P, 2 * P]), sb("rest_p", [P, P])

        ps = [stack.enter_context(nc.psum_tensor(f"ps{i}", [P, GT, P], F32)) for i in range(8)]

        block = stack.enter_context(nc.Block())

        def tile(t, buffer, n=1):
            return buffer[:, t:t + n, :] if isinstance(t, int) else buffer[:, bass.ds(t, n), :]

        class Chain:
            def __init__(self, eng, name):
                self.eng, self.sem = eng, sem(name)
                self.base, self.n = 0, 0

            def link(self, instruction, carried=False):
                self.n += 1
                instruction.then_inc(self.sem, 1)
                self.eng.wait_ge(self.sem, self.base + self.n)
                if carried and not isinstance(self.base, int):
                    carry_wait(self.eng)

            def loop(self, i, step):
                self.before, self.start = (self.base, self.n), self.n
                self.base = self.base + i * step
                self.step = step

            def end(self, turns):
                assert self.n - self.start == self.step, self.n - self.start
                self.base, self.n = self.before[0] + turns * self.step, self.before[1]

        def carry_wait(eng):
            if eng is nc.vector:
                eng.tensor_copy(carrier[:], neghalf[:, 0:1])
            else:
                eng.tensor_tensor(carrier_p[:], neghalf[:, 0:1], neghalf[:, 0:1], ALU.add)

        @block.sync
        def _(sp):
            def load(dst, src, name):
                sp.dma_start(dst, src).then_inc(sem(name), 16)

            xv = x.rearrange("b p d -> p b d")
            cv = ctxT.rearrange("d (b p) -> d b p", b=B)
            for g in range(G):
                load(xs[:, GT * g:GT * (g + 1), :], xv[:, GT * g:GT * (g + 1), :], f"x_in{g}")
                if g == 0:
                    load(ctxg[:], cv[:, 0:GT, :], "ctxg_in")
                    load(wk0[:], Wk0, "a_in")
                    load(wv0[:], Wv0, "a_in")
                    load(wq0[:], Wq0, "a_in")
                    load(bq0c[:], bq0.rearrange("(p a) -> p a", a=1), "a_in")
                    load(bk0c[:], bk0.rearrange("(p a) -> p a", a=1), "a_in")
                    load(bv0r[:], stretch(bv0.rearrange("(a n) -> a n", a=1), 0, P), "a_in")
            load(wg[:], Wg, "b_in")
            load(w1, W1.rearrange("p (e f n) -> p e f n", e=E8, f=F0), "b_in")
            load(w2, W2.rearrange("p (e f n) -> p e f n", e=E8, f=F0), "b_in")
            load(wq1[:], Wq1.rearrange("p (c n) -> p c n", c=PAIRS), "c_in")
            load(wk1[:], Wk1.rearrange("p (c n) -> p c n", c=PAIRS), "c_in")
            load(wv1[:], Wv1.rearrange("p (c n) -> p c n", c=PAIRS), "c_in")
            load(wo1[:], Wo1.rearrange("p (c n) -> p c n", c=PAIRS), "c_in")
            load(bo1r[:], stretch(bo1.rearrange("(a n) -> a n", a=1), 0, P), "c_in")
            load(gwis[:], gwi.rearrange("p (c n) -> p c n", c=F1), "d_in")
            load(gwos[:], gwo.rearrange("p (c n) -> p c n", c=F1), "d_in")
            load(gbic[:], gbi, "d_in")
            load(gbor[:], stretch(gbo.rearrange("(a n) -> a n", a=1), 0, P), "d_in")
            load(ewis[:], ewi.rearrange("p (e f n) -> p e f n", e=E8, f=F1), "e_in")
            load(ewos[:], ewo.rearrange("p (e f n) -> p e f n", e=E8, f=F1), "e_in")
            load(ebic[:], ebi.rearrange("p (e f) -> p e f", e=E8), "e_in")
            load(ebos[:], ebo, "e_in")
            with sp.Fori(0, G - 1) as g:
                sp.wait_ge(sem("A_v"), g + 1)
                load(ctxg[:], cv[:, bass.ds(GT * g + GT, GT), :], "ctxg_in")
            for b in range(2):
                load(ctxb[b][:], cv[:, b, :], f"ctx_in{b}")
            with sp.Fori(0, B // 2 - 1) as i:
                for par in range(2):
                    sp.wait_ge(sem("C_v1"), 2 * i + par + 1)
                    load(ctxb[par][:], cv[:, bass.ds(2 * i + 2 + par, 1), :], f"ctx_in{par}")
            sp.wait_ge(sem("E_count"), 1)
            n_chunks = sp.value_load(nchi[0:1, 0:1], min_val=1, max_val=B // 2)
            ov = out.rearrange("b p d -> p b d")
            for q in range(G):
                sp.wait_ge(sem("E_x"), G * n_chunks + q + 1)
                sp.dma_start(ov[:, GT * q:GT * (q + 1), :], xs[:, GT * q:GT * (q + 1), :]).then_inc(sem("stored"), 16)
            sp.wait_ge(sem("stored"), 16 * G)

        @block.gpsimd
        def _(pool):
            pool.memset(neghalf[:], -0.5).then_inc(sem("filled"), 1)
            pool.memset(var[:], 1.0).then_inc(sem("filled"), 1)
            pool.memset(ones[:], 1.0).then_inc(sem("const"), 1)
            pool.memset(ident[:], 0.0).then_inc(sem("const"), 1)
            pool.memset(lnalpha[:], LN_ALPHA).then_inc(sem("const"), 1)
            for i in range(2):
                pool.memset(v[i][:, :, DH:DH + 1], 1.0).then_inc(sem("const"), 1)
            pool.iota(iota[:], pattern=[[1, P]], base=0, channel_multiplier=0,
                      allow_small_or_imprecise_dtypes=True).then_inc(sem("const"), 1)
            pool.iota(iotab[:], pattern=[[1, SLOTS]], base=0, channel_multiplier=0,
                      allow_small_or_imprecise_dtypes=True).then_inc(sem("const"), 1)
            pool.wait_ge(sem("const"), 7)
            pool.affine_select(out=ident[:], in_=ident[:], compare_op=ALU.not_equal, fill=1.0, base=0,
                               pattern=[[-1, P]], channel_multiplier=1).then_inc(sem("const"), 1)
            pool.wait_ge(sem("const"), 8)
            pool.tensor_copy(identb[:], ident[:]).then_inc(sem("const"), 1)
            pool.affine_select(out=before[:], in_=ones[:], compare_op=ALU.is_gt, fill=0.0, base=0,
                               pattern=[[1, P]], channel_multiplier=-1).then_inc(sem("const"), 1)

            def power(index):
                pool.wait_ge(sem("ln_var"), index + 1)
                pool.tensor_tensor(rstd[:], var[:], neghalf[:], ALU.pow).then_inc(sem("ln_rstd"), 1)

            pool.wait_ge(sem("filled"), 2)
            with pool.Fori(0, 2 * G) as n:
                power(n)

            def bias(b):
                pool.wait_ge(sem("C_ln"), b + 1)
                pool.tensor_tensor(tile(b, xs), tile(b, xs), bo1r[:].unsqueeze(1), ALU.add)\
                    .then_inc(sem("C_biased"), 1)

            chain = Chain(pool, "pool")

            def keep(d, par):
                pool.wait_ge(sem("C_ln"), d + 4)
                hi, mid, lo = (tile(d, xn3[:, k, :, :]) for k in range(3))
                xd, rp = xnD[par][:].unsqueeze(1), rest_p[:].unsqueeze(1)
                chain.link(pool.tensor_copy(hi, xd), carried=True)
                chain.link(pool.tensor_tensor(rp, xd, hi, ALU.subtract))
                chain.link(pool.tensor_copy(mid, rp), carried=True)
                chain.link(pool.tensor_tensor(rp, rp, mid, ALU.subtract))
                pool.tensor_copy(lo, rp).then_inc(sem("D_kept"), 1)
                pool.wait_ge(sem("D_kept"), d + 1)

            pool.wait_ge(sem("c_in"), 16 * 5)
            first = 2 * G
            for n in range(3):
                power(first + n)
                bias(n)
            with pool.Fori(0, (B - 4) // 2) as i:
                chain.loop(i, 2 * 4)
                for k in range(2):
                    power(first + 2 * i + 3 + k)
                    bias(2 * i + 3 + k)
                    keep(2 * i + k, k)
            chain.end((B - 4) // 2)
            power(first + B - 1)
            bias(B - 1)
            keep(B - 4, 0)
            for d in range(B - 3, B):
                power(first + d + 3)
                keep(d, d % 2)

        CONST = 10

        @block.tensor
        def _(pe):
            def mm(dst, lhsT, rhs, start=True, stop=True):
                return pe.matmul(dst, lhsT, rhs, start=start, stop=stop)

            pe.sem_inc(sem("B_y"), 2)
            pe.wait_ge(sem("const"), CONST)
            def a_project_k(n):
                pe.wait_ge(sem("A_ln"), n + 1)
                wait(pe, "B_lshift", n)
                for t in range(GT):
                    last = pe.transpose(ps[6][:, t, :], xng[:, t, :], ident[:])
                last.then_inc(sem("A_tr"), 1)
                pe.wait_ge(sem("ctxg_in"), 16 * n + 16)
                wait(pe, "B_xT", n)
                mm(ps[7][:], wk0[:], ctxg[:]).then_inc(sem("A_k"), 1)

            def a_project_qv(n):
                pe.wait_ge(sem("A_xT"), n + 1)
                mm(ps[6][:], wq0[:], xTg[:]).then_inc(sem("A_q"), 1)
                pe.wait_ge(sem("A_k_out"), n + 1)
                for t in range(GT):
                    last = mm(ps[7][:, t, :], ctxg[:, t, :], wv0[:])
                last.then_inc(sem("A_v"), 1)

            def a_scores(n):
                pe.wait_ge(sem("A_q_out"), n + 1)
                for t in range(GT):
                    last = mm(ps[6][:, t, :], qT[0][:, t, :], kT[0][:, t, :])
                last.then_inc(sem("A_s"), 1)

            def a_transpose(n):
                pe.wait_ge(sem("A_exp"), n + 1)
                pe.wait_ge(sem("A_v_out"), n + 1)
                for t in range(GT):
                    last = pe.transpose(ps[7][:, t, :], prob[0][:, t, :], ident[:])
                last.then_inc(sem("A_ptr"), 1)

            def a_attend(n):
                pe.wait_ge(sem("A_pT"), n + 1)
                for t in range(GT):
                    last = mm(ps[6][:, t, :], probT[0][:, t, :], vA[:, t, :])
                last.then_inc(sem("A_o"), 1)

            def b_transpose(n):
                pe.wait_ge(sem("B_ln"), n + 1)
                for t in range(GT):
                    last = pe.transpose(ps[7][:, t, :], xng[:, t, :], ident[:])
                last.then_inc(sem("B_tr"), 1)

            def b_logits(n):
                pe.wait_ge(sem("B_xT"), n + 1)
                for t in range(GT):
                    last = mm(ps[6][:, t, 0:E8], xTg[:, t, :], wg[:])
                last.then_inc(sem("B_l"), 1)

            def hidden(g, e):
                pe.wait_ge(sem("B_relu"), E8 * g + e + 1)
                for f in range(F0):
                    last = mm(ps[F0 * (e % 2) + f][:], w1[:, e, f, :], tile(GT * g, xT_all, GT))
                    last.then_inc(sem("B_h"), 1)

            def output(g, e):
                pe.wait_ge(sem("B_relu"), 2 + E8 * g + e + 1)
                pe.wait_ge(sem("B_y_out"), E8 * g + e + 1)
                for t in range(GT):
                    for f in range(F0):
                        last = mm(ps[4 + e % 2][:, t, :], hidB[e % 2][f][:, P * t:P * t + P], w2[:, e, f, :],
                                  start=f == 0, stop=f == F0 - 1)
                last.then_inc(sem("B_y"), 1)

            def experts(g, n=None):
                steps = {0: a_project_k, 1: a_project_qv, 2: a_scores, 4: a_transpose, 5: a_attend, 6: b_transpose, 7: b_logits}
                hidden(g, 0)
                for e in range(E8):
                    if e + 1 < E8:
                        hidden(g, e + 1)
                    output(g, e)
                    if n is not None and e in steps:
                        steps[e](n)

            pe.wait_ge(sem("a_in"), 16 * 6)
            for step in (a_project_k, a_project_qv, a_scores, a_transpose, a_attend, b_transpose):
                step(0)
            pe.wait_ge(sem("b_in"), 16 * 3)
            b_logits(0)
            with pe.Fori(0, G - 1) as g:
                experts(g, g + 1)
            experts(G - 1)
            pe.wait_ge(sem("B_y_out"), 2 + E8 * G)

            def transposes_p(b, s, u):
                for a in range(2):
                    pe.wait_ge(sem(f"C_exp{u}{a}"), b + 1)
                    if u == 0:
                        pe.wait_ge(sem(f"C_pT1{a}"), b) if not isinstance(b, int) or b > 0 else None
                    else:
                        wait(pe, f"C_hT{a}", b)
                        wait(pe, f"C_pT0{a}", b + 1)
                    for h in range(GT):
                        last = pe.transpose(ps[4 + a][:, h, :], prob[2 * u + a][:, h, :], ident[:])
                    last.then_inc(sem(f"C_ptr{u}{a}"), 1)

            def attend(b, s, u):
                for a in range(2):
                    pe.wait_ge(sem(f"C_pT{u}{a}"), b + 1)
                    if a == 0 and u == 0:
                        pe.wait_ge(sem("C_v0_out"), b + 1)
                        pe.wait_ge(sem("C_v1_out"), b + 1)
                    wait(pe, f"C_hd{1 - u}{a}", b if u == 0 else b + 1)
                    for h in range(GT):
                        last = mm(ps[6 + a][:, h, 0:DH + 1], probT[2 * u + a][:, h, :],
                                  v[s][:, 2 * GT * u + 2 * h + a, :])
                    last.then_inc(sem(f"C_o{u}{a}"), 1)

            def scores(b, s, u):
                if u == 0:
                    for name in ("C_q0_out", "C_q1_out", "C_k0_out", "C_k1_out"):
                        pe.wait_ge(sem(name), b + 1)
                for a in range(2):
                    wait(pe, f"C_shift{1 - u}{a}", b if u == 0 else b + 1)
                for h in range(GT):
                    for a in range(2):
                        last = mm(ps[2 + a][:, h, :], qT[s][DH * a:DH * (a + 1), GT * u + h, :],
                                  kT[s][DH * a:DH * (a + 1), GT * u + h, :])
                last.then_inc(sem(f"C_s{u}"), 1)

            def transpose_x(b, s, d=True, x=True):
                pe.wait_ge(sem("C_ln"), b + 1)
                wait(pe, "C_v0_out", b if x else B)
                if not x:
                    wait(pe, "C_xT", b)
                if d:
                    last = pe.transpose(ps[0][:, 1, :], xnD[1 - s][:], ident[:])
                if x:
                    last = pe.transpose(ps[0][:, 0, :], xn[s][:], ident[:])
                last.then_inc(sem("C_xtr"), 1)

            def project_q(b, s):
                pe.wait_ge(sem("C_xT"), b + 1)
                wait(pe, "C_v1_out", b)
                for c, bank in ((0, 1), (1, 0)):
                    for i in range(GT):
                        last = mm(ps[bank][:, i, :], wq1[:, GT * c + i, :], xT[s][:])
                    last.then_inc(sem(f"C_q{c}"), 1)

            def project_k(b, s, n_ctx):
                pe.wait_ge(sem(f"ctx_in{s}"), n_ctx)
                for c, bank in ((0, 1), (1, 0)):
                    pe.wait_ge(sem(f"C_q{c}_out"), b + 1)
                    for i in range(GT):
                        last = mm(ps[bank][:, i, :], wk1[:, GT * c + i, :], ctxb[s][:])
                    last.then_inc(sem(f"C_k{c}"), 1)

            def project_v(b, s, after_out):
                for c, bank in ((0, 0), (1, 1)):
                    if c == 0:
                        pe.wait_ge(sem("C_k1_out"), b + 1)
                    else:
                        wait(pe, "C_k0_out", b + 1)
                        wait(pe, "C_x", after_out)
                    mm(ps[bank][:], ctxb[s][:], wv1[:, GT * c:GT * (c + 1), :]).then_inc(sem(f"C_v{c}"), 1)

            def transpose_heads(b, s):
                for a in range(2):
                    for u in range(2):
                        pe.wait_ge(sem(f"C_hd{u}{a}"), b + 1)
                for a in range(2):
                    wait(pe, f"C_pT0{a}", b + 2 if not isinstance(b, int) or b < B - 1 else B)
                    wait(pe, f"C_pT1{a}", b + 1)
                    for i in range(GT):
                        c = GT * a + i
                        last = pe.transpose(ps[4 + a][:, i, :], heads[s][:, 2 * c:2 * c + 2, :], ident[:])
                    last.then_inc(sem(f"C_htr{a}"), 1)

            def project_out(b, has_next):
                pe.wait_ge(sem("C_hT0"), b + 1)
                pe.wait_ge(sem("C_hT1"), b + 1)
                if has_next:
                    pe.wait_ge(sem("C_k0_out"), b + 3)
                else:
                    pe.wait_ge(sem("C_v1_out"), B)
                    wait(pe, "C_x", b)
                for c in range(PAIRS):
                    last = mm(ps[1][:, 0, :], headsT[:, c, :], wo1[:, c, :], start=c == 0, stop=c == PAIRS - 1)
                last.then_inc(sem("C_out"), 1)

            def body(b, s, n_ctx, first=False, last=False):
                scores(b, s, 0)
                if not first:
                    transposes_p(b - 1, 1 - s, 1)
                transpose_x(b + 1, 1 - s, d=not isinstance(b, int) or b >= 2, x=not last)
                if not first:
                    attend(b - 1, 1 - s, 1)
                if not last:
                    project_q(b + 1, 1 - s)
                transposes_p(b, s, 0)
                scores(b, s, 1)
                attend(b, s, 0)
                if not first:
                    transpose_heads(b - 1, 1 - s)
                if not last:
                    project_k(b + 1, 1 - s, n_ctx)
                if not first:
                    project_out(b - 1, not last)
                if not last:
                    project_v(b + 1, 1 - s, b)

            pe.wait_ge(sem("c_in"), 16 * 5)
            transpose_x(0, 0, d=False)
            project_q(0, 0)
            project_k(0, 0, 16)
            project_v(0, 0, 0)
            body(0, 0, 16, first=True)
            body(1, 1, 32)
            with pe.Fori(0, B // 2 - 2) as i:
                body(2 * i + 2, 0, 16 * i + 32)
                body(2 * i + 3, 1, 16 * i + 48)
            body(B - 2, 0, 16 * (B // 2))
            body(B - 1, 1, None, last=True)
            transposes_p(B - 1, 1, 1)
            attend(B - 1, 1, 1)
            transpose_heads(B - 1, 1)
            project_out(B - 1, False)

            transpose_x(B + 1, 1, x=False)
            transpose_x(B + 2, 0, x=False)

            pe.wait_ge(sem("d_in"), 16 * 4)
            pe.wait_ge(sem("C_xT"), B + 3)
            pe.wait_ge(sem("C_x"), B)
            with pe.Fori(0, G // 2) as i:
                for k in range(2):
                    pe.wait_ge(sem("D_u"), F1 * (2 * i + k + 1))
                    pe.wait_ge(sem("D_glog"), 2 * i + k + 1)
                    for f in range(F1):
                        mm(ps[F1 * k + f][:], gwis[:, f, :], tile(2 * GT * i + GT * k, xT_all, GT)).then_inc(sem("D_h"), 1)
                for k in range(2):
                    pe.wait_ge(sem("D_selu"), 2 + F1 * (2 * i + k + 1))
                    for t in range(GT):
                        for f in range(F1):
                            last = mm(ps[F1 * k][:, t, :], hidD[k][f][:, P * t:P * t + P],
                                      gwos[:, f, :], start=f == 0, stop=f == F1 - 1)
                    last.then_inc(sem("D_l"), 1)

            pe.wait_ge(sem("E_rowsum"), 1)
            mm(ps[5][:, 0, 0:1], before[:], rowsum[:])
            mm(ps[5][:, 1, 0:1], ones[:], rowsum[:]).then_inc(sem("E_ranked"), 1)
            pe.wait_ge(sem("e_in"), 16 * 4)
            pe.wait_ge(sem("D_kept"), B)
            pe.wait_ge(sem("E_count"), 1)
            n_chunks = pe.value_load(nchi[0:1, 0:1], min_val=1, max_val=B // 2)
            xcb, wcb = ps[6][:, 0:2, :], ps[7][:, 0, 0:2 * 3 * E8].rearrange("p (h k) -> p h k", h=2)

            def transpose_pick(c, q):
                pe.wait_ge(sem("E_xc"), c + 1)
                if q > 0:
                    pe.wait_ge(sem("E_pickT"), G * c + q)
                bank = ps[6][:].rearrange("p t n -> p (t n)").bitcast(BF16).rearrange("p (t h n) -> p t h n", t=GT, h=2)
                for t in range(GT):
                    for h in range(2):
                        last = pe.transpose(bank[:, t, h, :], pick[:, GT * q + t, P * h:P * h + P], identb[:])
                last.then_inc(sem("E_ptr"), 1)

            with pe.Fori(0, n_chunks) as c:
                pe.wait_ge(sem("E_x"), G * (c + 1))
                for t in range(B):
                    if t % GT == 0:
                        pe.wait_ge(sem("E_pick"), G * c + t // GT + 1)
                    for k in range(3):
                        last = mm(xcb, xn3[:, k, t, :], pick[:, t, :], start=t == 0 and k == 0, stop=t == B - 1 and k == 2)
                last.then_inc(sem("E_gx"), 1)
                for h in range(2):
                    for t in range(B):
                        last = mm(wcb[:, h, :], pick[:, t, P * h:P * h + P], w3[:, t, :, :], start=t == 0, stop=t == B - 1)
                last.then_inc(sem("E_gw"), 1)

                def hidden(e):
                    pe.wait_ge(sem("E_u"), E8 * c + e + 1)
                    for f in range(F1):
                        last = mm(ps[2 * (e % 2) + f // 2][:, 2 * (f % 2):2 * (f % 2) + 2, :], ewis[:, e, f, :], xc[:])
                    last.then_inc(sem("E_h"), 1)

                def output(e):
                    pe.wait_ge(sem("E_hid"), 2 + E8 * c + e + 1)
                    pe.wait_ge(sem("E_y_out"), E8 * c + e + 1)
                    for h in range(2):
                        for f in range(F1):
                            last = mm(ps[4 + e % 2][:, h, :], hid[e % 2][:, f, P * h:P * h + P], ewos[:, e, f, :],
                                      start=f == 0, stop=f == F1 - 1)
                    last.then_inc(sem("E_y"), 1)

                pe.wait_ge(sem("E_xc"), c + 1)
                hidden(0)
                pe.wait_ge(sem("E_wc"), c + 1)
                for h in range(2):
                    last = pe.transpose(ps[7][0:E8, 1 + h, :], wc[:, h, :], ident[:])
                last.then_inc(sem("E_wtr"), 1)
                hidden(1)
                pe.wait_ge(sem("E_wcT"), c + 1)
                for h in range(2):
                    last = mm(ps[7][:, h, :], wcT[:, h, :], ebos[:])
                last.then_inc(sem("E_bias"), 1)
                output(0)
                for e in range(2, E8):
                    hidden(e)
                    if e % 2 == 0:
                        q = e // 2 - 1
                        transpose_pick(c, q)
                    output(e - 1)
                transpose_pick(c, G - 1)
                output(E8 - 1)
                pe.wait_ge(sem("E_y3"), c + 1)
                pe.wait_ge(sem("E_pickT"), G * (c + 1))
                for q in range(G):
                    pe.wait_ge(sem("E_x"), G * c + q + 3)
                    for t in range(GT):
                        for h in range(2):
                            for k in range(3):
                                last = mm(ps[6 + q % 2][:, t, :], pickT[:, GT * q + t, h, :], y3[:, k, h, :],
                                          start=h == 0 and k == 0, stop=h == 1 and k == 2)
                    last.then_inc(sem("E_back"), 1)

        @block.scalar
        def _(act):
            for name, n in (("B_relu", 2), ("D_u", 2 * F1), ("E_u", 2)):
                act.sem_inc(sem(name), n)

            def a_project_k(n):
                act.wait_ge(sem("A_tr"), n + 1)
                act.copy(xTg[:], ps[6][:]).then_inc(sem("A_xT"), 1)
                act.wait_ge(sem("A_k"), n + 1)
                act.activation(kT[0][:, 0:GT, :], ps[7][:], ACT.Identity, bias=bk0c[:]).then_inc(sem("A_k_out"), 1)

            def a_project_q(n):
                act.wait_ge(sem("A_q"), n + 1)
                act.activation(qT[0][:, 0:GT, :], ps[6][:], ACT.Identity, bias=bq0c[:]).then_inc(sem("A_q_out"), 1)

            def a_exp(n):
                act.wait_ge(sem("A_shift"), n + 1)
                act.activation(prob[0][:], shifted[0][:], ACT.Exp, scale=P ** -0.5).then_inc(sem("A_exp"), 1)

            def a_copy_pT(n):
                act.wait_ge(sem("A_ptr"), n + 1)
                act.copy(probT[0][:], ps[7][:]).then_inc(sem("A_pT"), 1)

            def b_copy_xT(n):
                act.wait_ge(sem("B_tr"), n + 1)
                act.copy(xTg[:], ps[7][:]).then_inc(sem("B_xT1"), 1)
                act.copy(tile(GT * n, xT_all, GT), ps[7][:]).then_inc(sem("B_xT"), 1)

            def b_exp(n):
                act.wait_ge(sem("B_lshift"), n + 1)
                act.activation(lg[:], rt1[:], ACT.Exp).then_inc(sem("B_lexp"), 1)

            def relu(g, e):
                act.wait_ge(sem("B_y"), E8 * g + e + 1)
                for f in range(F0):
                    act.wait_ge(sem("B_h"), F0 * (E8 * g + e) + f + 1)
                    last = act.activation(hidB[e % 2][f], ps[F0 * (e % 2) + f][:].rearrange("p t n -> p (t n)"), ACT.Relu)
                last.then_inc(sem("B_relu"), 1)

            def experts(g, n=None):
                steps = {1: a_project_k, 2: a_project_q, 4: a_exp, 5: a_copy_pT, 7: b_copy_xT}
                for e in range(E8):
                    relu(g, e)
                    if n is not None and e in steps:
                        steps[e](n)
                if n is not None:
                    b_exp(n)

            act.wait_ge(sem("a_in"), 16 * 6)
            for step in (a_project_k, a_project_q, a_exp, a_copy_pT, b_copy_xT, b_exp):
                step(0)
            with act.Fori(0, G - 1) as g:
                experts(g, g + 1)
            experts(G - 1)

            def copy_pT(b, u):
                for a in range(2):
                    act.wait_ge(sem(f"C_ptr{u}{a}"), b + 1)
                    wait(act, f"C_o{u}{a}", b)
                    act.copy(probT[2 * u + a][:], ps[4 + a][:]).then_inc(sem(f"C_pT{u}{a}"), 1)

            def exp(b, u):
                for a in range(2):
                    act.wait_ge(sem(f"C_shift{u}{a}"), b + 1)
                    wait(act, f"C_ptr{u}{a}", b)
                    act.activation(prob[2 * u + a][:], shifted[a][:], ACT.Exp, scale=DH ** -0.5)\
                        .then_inc(sem(f"C_exp{u}{a}"), 1)

            def copy_x(b, s, d=True, x=True):
                act.wait_ge(sem("C_xtr"), b + 1)
                if d:
                    last = act.copy(tile(b - 3, xT_all), ps[0][:, 1:2, :])
                if x:
                    wait(act, "C_q1", b - 1)
                    last = act.copy(xT[s][:], ps[0][:, 0, :])
                last.then_inc(sem("C_xT"), 1)

            def copy_q(b, s):
                for c, bank in ((0, 1), (1, 0)):
                    act.wait_ge(sem(f"C_q{c}"), b + 1)
                    wait(act, "C_s1", b - 1)
                    act.copy(qT[s][:, GT * c:GT * (c + 1), :], ps[bank][:]).then_inc(sem(f"C_q{c}_out"), 1)

            def copy_k(b, s):
                act.wait_ge(sem("C_k0"), b + 1)
                wait(act, "C_s1", b - 1)
                act.copy(kT[s][:, 0:GT, :], ps[1][:]).then_inc(sem("C_k0_out"), 1)

            def copy_v(b, s):
                act.wait_ge(sem("C_v0"), b + 1)
                wait(act, "C_o11", b - 1)
                act.copy(v[s][:, 0:8, 0:DH], ps[0][:].rearrange("p t (h d) -> p (t h) d", d=DH)).then_inc(sem("C_v0_out"), 1)

            def copy_heads(b):
                for a in range(2):
                    act.wait_ge(sem(f"C_htr{a}"), b + 1)
                    wait(act, "C_out", b)
                    act.copy(headsT[:, GT * a:GT * (a + 1), :], ps[4 + a][:]).then_inc(sem(f"C_hT{a}"), 1)

            def body(b, s, first=False, last=False):
                if not first:
                    copy_pT(b - 1, 1)
                copy_x(b + 1, 1 - s, d=not isinstance(b, int) or b >= 2, x=not last)
                exp(b, 0)
                if not last:
                    copy_q(b + 1, 1 - s)
                copy_pT(b, 0)
                exp(b, 1)
                if not first:
                    copy_heads(b - 1)
                if not last:
                    copy_k(b + 1, 1 - s)
                    copy_v(b + 1, 1 - s)

            copy_x(0, 0, d=False)
            copy_q(0, 0)
            copy_k(0, 0)
            copy_v(0, 0)
            body(0, 0, first=True)
            body(1, 1)
            with act.Fori(0, B // 2 - 2) as i:
                body(2 * i + 2, 0)
                body(2 * i + 3, 1)
            body(B - 2, 0)
            body(B - 1, 1, last=True)
            copy_pT(B - 1, 1)
            copy_heads(B - 1)

            copy_x(B + 1, 1, x=False)
            copy_x(B + 2, 0, x=False)

            with act.Fori(0, G // 2) as i:
                for k in range(2):
                    for f in range(F1):
                        n = F1 * (2 * i + k) + f
                        act.wait_ge(sem("D_h"), n + 1)
                        act.wait_ge(sem("D_selu"), n + 1)
                        u, e = act_u[f % 2][:, 0:F0, :], act_e[f % 2][:, 0:F0, :]
                        act.activation(u.rearrange("p a n -> p (a n)"), ps[F1 * k + f][:].rearrange("p t n -> p (t n)"),
                                       ACT.Identity, bias=gbic[:, f:f + 1]).then_inc(sem("D_u"), 1)
                        act.wait_ge(sem("D_u"), n + 2 * F1 + 1)
                        act.activation(e, u, ACT.Exp, bias=lnalpha[:]).then_inc(sem("D_exp"), 1)

            act.wait_ge(sem("E_count"), 1)
            n_chunks = act.value_load(nchi[0:1, 0:1], min_val=1, max_val=B // 2)
            with act.Fori(0, n_chunks) as c:
                def hidden(e):
                    act.wait_ge(sem("E_h"), E8 * c + e + 1)
                    act.wait_ge(sem("E_hid"), E8 * c + e + 1)
                    for f in range(F1):
                        last = act.activation(act_u[e % 2][:, f, :], ps[2 * (e % 2) + f // 2][:, 2 * (f % 2):2 * (f % 2) + 2, :],
                                              ACT.Identity, bias=ebic[:, e, f:f + 1])
                    last.then_inc(sem("E_u"), 1)
                    act.wait_ge(sem("E_u"), 2 + E8 * c + e + 1)
                    act.activation(act_e[e % 2][:], act_u[e % 2][:], ACT.Exp, bias=lnalpha[:]).then_inc(sem("E_e"), 1)

                def copy_pick(q):
                    act.wait_ge(sem("E_ptr"), G * c + q + 1)
                    bank = ps[6][:].rearrange("p t n -> p (t n)").bitcast(BF16).rearrange("p (t h n) -> p t h n", t=GT, h=2)
                    act.copy(pickT[:, GT * q:GT * (q + 1), :, :], bank).then_inc(sem("E_pickT"), 1)

                hidden(0)
                hidden(1)
                for e in range(2, E8):
                    hidden(e)
                    if e % 2 == 0:
                        copy_pick(e // 2 - 1)
                copy_pick(G - 1)

        @block.vector
        def _(dve):
            chain = Chain(dve, "dve")
            link = chain.link

            def layer_norm(tiles, done, index):
                if not isinstance(index, int):
                    carry_wait(dve)
                for t, (src, _) in enumerate(tiles):
                    last = dve.bn_stats(stats[:, t, :], src)
                link(last, carried=True)
                for t in range(len(tiles)):
                    last = dve.bn_aggr(mv[:, t, :], stats[:, t, :])
                link(last)
                dve.tensor_scalar(var[:, 0:len(tiles)], mv[:, 0:len(tiles), 1], EPS, None, ALU.add).then_inc(sem("ln_var"), 1)
                dve.wait_ge(sem("ln_rstd"), index + 1)
                for t, (src, dst) in enumerate(tiles):
                    last = dve.tensor_scalar(dst, src, mv[:, t, 0:1], rstd[:, t:t + 1], ALU.subtract, ALU.mult)
                last.then_inc(sem(done), 1)

            def shift(bank, k, wait_free, done):
                link(dve.tensor_reduce(smax[k][:], ps[bank][:], AX.X, ALU.max))
                wait_free()
                dve.tensor_tensor(shifted[k][:], ps[bank][:], stretch(smax[k][:].unsqueeze(2), 2, P), ALU.subtract)\
                    .then_inc(sem(done), 1)

            def find_top(values):
                for t in range(GT):
                    last = dve.max(top[:, t, :], values(t))
                link(last, carried=True)
                for t in range(GT):
                    last = dve.max_index(topi[:, t, :], top[:, t, :], values(t))
                link(last)

            def place(value, index, r1, r2, r3, n, dst):
                link(dve.tensor_tensor(r3.unsqueeze(2), value[:, :, 0:1], value[:, :, 1:2], ALU.add))
                link(dve.reciprocal(r3, r3))
                link(dve.tensor_tensor(value[:, :, 0:2], value[:, :, 0:2], stretch(r3.unsqueeze(2), 2, 2), ALU.mult))
                eight = stretch(iota[:, 0:E8].unsqueeze(1), 1, n)
                for k, r in ((0, r1), (1, r2)):
                    last = dve.tensor_tensor(r, eight, stretch(index[:, :, k:k + 1], 2, E8), ALU.is_equal)
                link(last)
                for k, r in ((0, r1), (1, r2)):
                    last = dve.tensor_tensor(r, r, stretch(value[:, :, k:k + 1], 2, E8), ALU.mult)
                link(last)
                return dve.tensor_tensor(dst, r1, r2, ALU.add)

            for name, n in (("B_y_out", 2), ("D_glog", 2), ("D_selu", 2),
                            ("E_hid", 2), ("E_y_out", 2), ("E_x", G)):
                dve.sem_inc(sem(name), n)
            dve.wait_ge(sem("filled"), 2)

            def group(n):
                return [(tile(GT * n + t, xs), xng[:, t:t + 1, :]) for t in range(GT)]

            def a_norm(n):
                wait(dve, "B_tr", n)
                layer_norm(group(n), "A_ln", 2 * n)

            def a_copy_v(n):
                dve.wait_ge(sem("A_v"), n + 1)
                dve.tensor_tensor(vA[:], ps[7][:], stretch(bv0r[:].unsqueeze(1), 1, GT), ALU.add)\
                    .then_inc(sem("A_v_out"), 1)

            def a_shift(n):
                dve.wait_ge(sem("A_s"), n + 1)
                shift(6, 0, lambda: None, "A_shift")

            def a_sum(n):
                dve.wait_ge(sem("A_exp"), n + 1)
                link(dve.tensor_reduce(ssum[0][:], prob[0][:], AX.X, ALU.add))
                link(dve.reciprocal(ssum[0][:], ssum[0][:]))

            def a_add(n):
                dve.wait_ge(sem("A_o"), n + 1)
                for t in range(GT):
                    xt = tile(GT * n + t, xs)
                    last = dve.scalar_tensor_tensor(xt, ps[6][:, t:t + 1, :], ssum[0][:, t:t + 1], xt, ALU.mult, ALU.add)
                last.then_inc(sem("A_x"), 1)
                dve.wait_ge(sem("A_x"), n + 1)
                layer_norm(group(n), "B_ln", 2 * n + 1)

            def b_route(n):
                dve.wait_ge(sem("B_l"), n + 1)
                bank = ps[6][:, :, 0:E8]
                link(dve.tensor_reduce(smax[0][:], bank, AX.X, ALU.max))
                dve.tensor_tensor(rt1[:], bank, stretch(smax[0][:].unsqueeze(2), 2, E8), ALU.subtract)\
                    .then_inc(sem("B_lshift"), 1)
                dve.wait_ge(sem("B_lexp"), n + 1)
                link(dve.tensor_reduce(rsc[:], lg[:], AX.X, ALU.add))
                link(dve.reciprocal(rsc[:], rsc[:]))
                link(dve.tensor_tensor(lg[:], lg[:], stretch(rsc[:].unsqueeze(2), 2, E8), ALU.mult), carried=True)
                find_top(lambda t: lg[:, t, :])
                link(dve.tensor_copy(topf[:], topi[:]))
                link(place(top, topf, rt1[:], rt2[:], rsc[:], GT, tile(GT * n, w0, GT)))

            def experts(g, n=None):
                steps = {1: a_copy_v, 2: a_shift, 4: a_sum, 5: a_add}
                if n is not None:
                    a_norm(n)
                for e in range(E8):
                    dve.wait_ge(sem("B_y"), 2 + E8 * g + e + 1)
                    for t in range(GT):
                        xt = tile(GT * g + t, xs)
                        last = dve.scalar_tensor_tensor(xt, ps[4 + e % 2][:, t:t + 1, :], tile(GT * g + t, w0)[:, 0, e:e + 1],
                                                        xt, ALU.mult, ALU.add)
                    last.then_inc(sem("B_y_out"), 1)
                    dve.wait_ge(sem("B_y_out"), 2 + E8 * g + e + 1)
                    if n is not None and e in steps:
                        steps[e](n)
                if n is not None:
                    b_route(n)

            dve.wait_ge(sem("x_in0"), 16)
            a_norm(0)
            dve.wait_ge(sem("a_in"), 16 * 6)
            for step in (a_copy_v, a_shift, a_sum, a_add, b_route):
                step(0)
            for g in range(1, G):
                dve.wait_ge(sem(f"x_in{g}"), 16)
            with dve.Fori(0, G - 1) as g:
                chain.loop(g, 20)
                experts(g, g + 1)
            chain.end(G - 1)
            dve.wait_ge(sem("const"), CONST)
            layer_norm([(tile(0, xs), xn[0][:].unsqueeze(1))], "C_ln", 2 * G)
            layer_norm([(tile(1, xs), xn[1][:].unsqueeze(1))], "C_ln", 2 * G + 1)
            experts(G - 1)

            def norm(b, s, c=True, d=True):
                tiles = []
                if d:
                    wait(dve, "D_kept", b - 2)
                    tiles.append((tile(b - 1, xs), xnD[1 - s][:].unsqueeze(1)))
                if c:
                    tiles.append((tile(b + 2, xs), xn[s][:].unsqueeze(1)))
                wait(dve, "C_xtr", b + 1)
                layer_norm(tiles, "C_ln", 2 * G + b + 2)

            def shift_c(b, u):
                dve.wait_ge(sem(f"C_s{u}"), b + 1)
                for a in range(2):
                    shift(2 + a, a, lambda: wait(dve, f"C_exp{1 - u}{a}", b if u == 0 else b + 1), f"C_shift{u}{a}")

            def normalise(b, s, u):
                for a in range(2):
                    dve.wait_ge(sem(f"C_o{u}{a}"), b + 1)
                    bank = ps[6 + a]
                    link(dve.reciprocal(ssum[a][:].unsqueeze(2), bank[:, :, DH:DH + 1]))
                    if u == 0:
                        wait(dve, "C_htr1", b - 1)
                    dst = heads[s][:, 2 * GT * u:2 * GT * (u + 1), :].rearrange("p (i a) d -> p i a d", a=2)[:, :, a, :]
                    dve.tensor_tensor(dst, bank[:, :, 0:DH], stretch(ssum[a][:].unsqueeze(2), 2, DH), ALU.mult)\
                        .then_inc(sem(f"C_hd{u}{a}"), 1)

            def copy_k(b, s):
                dve.wait_ge(sem("C_k1"), b + 1)
                wait(dve, "C_s1", b - 1)
                dve.tensor_copy(kT[s][:, GT:2 * GT, :], ps[0][:]).then_inc(sem("C_k1_out"), 1)

            def copy_v(b, s):
                dve.wait_ge(sem("C_v1"), b + 1)
                wait(dve, "C_o11", b - 1)
                dve.tensor_copy(v[s][:, 8:16, 0:DH], ps[1][:].rearrange("p t (h d) -> p (t h) d", d=DH)).then_inc(sem("C_v1_out"), 1)

            def add_out(b):
                dve.wait_ge(sem("C_out"), b + 1)
                dve.wait_ge(sem("C_biased"), b + 1)
                xt = xs[:, b:b + 1, :] if isinstance(b, int) else xs[:, bass.ds(b, 1), :]
                dve.tensor_tensor(xt, ps[1][:, 0:1, :], xt, ALU.add).then_inc(sem("C_x"), 1)
                dve.wait_ge(sem("C_x"), b + 1)

            def body(b, s, first=False, last=False):
                shift_c(b, 0)
                if not first:
                    normalise(b - 1, 1 - s, 1)
                shift_c(b, 1)
                normalise(b, s, 0)
                if not last:
                    copy_k(b + 1, 1 - s)
                if not first:
                    add_out(b - 1)
                if not last:
                    copy_v(b + 1, 1 - s)
                norm(b, s, c=isinstance(b, int) is False or b < B - 2, d=not first)

            copy_k(0, 0)
            copy_v(0, 0)
            body(0, 0, first=True)
            body(1, 1)
            with dve.Fori(0, B // 2 - 2) as i:
                chain.loop(i, 2 * 10)
                body(2 * i + 2, 0)
                body(2 * i + 3, 1)
            chain.end(B // 2 - 2)
            body(B - 2, 0)
            body(B - 1, 1, last=True)
            normalise(B - 1, 1, 1)
            add_out(B - 1)
            norm(B, 0, c=False)

            dve.wait_ge(sem("d_in"), 16 * 4)
            with dve.Fori(0, G // 2) as i:
                chain.loop(i, 2 * (F1 + 4))
                for k in range(2):
                    for f in range(F1):
                        dve.wait_ge(sem("D_exp"), F1 * (2 * i + k) + f + 1)
                        u, e = act_u[f % 2][:, 0:F0, :], act_e[f % 2][:, 0:F0, :]
                        link(dve.tensor_scalar(e, e, SELU_ALPHA, -SELU_ALPHA, ALU.min, ALU.add))
                        dve.scalar_tensor_tensor(hidD[k][f].rearrange("p (a n) -> p a n", a=F0), u, 0.0, e, ALU.max, ALU.add)\
                            .then_inc(sem("D_selu"), 1)
                for k in range(2):
                    dve.wait_ge(sem("D_l"), 2 * i + k + 1)
                    dve.scalar_tensor_tensor(glog[k][:], ps[F1 * k][:], SELU_SCALE, stretch(gbor[:].unsqueeze(1), 1, GT),
                                             ALU.mult, ALU.add).then_inc(sem("D_glog"), 1)
                    dve.wait_ge(sem("D_glog"), 2 + 2 * i + k + 1)
                    carry_wait(dve)
                    find_top(lambda t: glog[k][:, t, :])
                    first = 2 * GT * i + GT * k
                    link(dve.tensor_copy(tile(first, topv16, GT), top[:, :, 0:2]))
                    link(dve.tensor_copy(tile(first, topi16, GT), topi[:, :, 0:2]))
            chain.end(G // 2)
            link(place(topv16[:], topi16[:], rt16[:, 0, :, :], rt16[:, 1, :, :], flag[:], B, w_e[:]))
            link(dve.tensor_scalar(rt16[:, 0, :, :], w_e[:], 0.0, None, ALU.not_equal))
            link(dve.tensor_reduce(flag[:], rt16[:, 0, :, :], AX.X, ALU.max))

            dve.tensor_reduce(rowsum[:], flag[:], AX.X, ALU.add).then_inc(sem("E_rowsum"), 1)
            link(dve.tensor_tensor_scan(ranks[:], ones[:, 0:B], flag[:], 0.0, ALU.mult, ALU.add))
            dve.wait_ge(sem("E_ranked"), 1)
            link(dve.tensor_scalar(ranks[:], ranks[:], ps[5][:, 0, 0:1], None, ALU.add))
            link(dve.tensor_tensor(pos[:], ranks[:], flag[:], ALU.mult))
            link(dve.tensor_scalar(pos[:], pos[:], -1.0, None, ALU.add))
            link(dve.tensor_copy(total[:], ps[5][:, 1, 0:1]))
            link(dve.tensor_scalar(ranks[:], iota[:, 0:B], float(SLOTS), total[:], ALU.mult, ALU.is_lt))
            link(dve.tensor_reduce(nchf[:], ranks[:], AX.X, ALU.add))
            link(dve.tensor_scalar(nchf[:], nchf[:], 1.0, None, ALU.max))
            dve.tensor_copy(nchi[:], nchf[:]).then_inc(sem("E_count"), 1)
            dve.wait_ge(sem("E_count"), 1)
            n_chunks = dve.value_load(nchi[0:1, 0:1], min_val=1, max_val=B // 2)

            def split(parts, value, r):
                link(dve.tensor_copy(parts[0], value))
                link(dve.tensor_tensor(r, value, parts[0], ALU.subtract))
                link(dve.tensor_copy(parts[1], r))
                link(dve.tensor_tensor(r, r, parts[1], ALU.subtract))
                return dve.tensor_copy(parts[2], r)

            link(split([w3[:, :, k, :] for k in range(3)], w_e[:], rt16[:, 0, :, :]))
            with dve.Fori(0, n_chunks) as c:
                chain.loop(c, 5 + E8 + 4)
                for t in range(B):
                    last = dve.tensor_scalar(pick[:, t, :], iotab[:], pos[:, t:t + 1], None, ALU.is_equal)
                    if t % GT == GT - 1:
                        last.then_inc(sem("E_pick"), 1)
                dve.wait_ge(sem("E_gx"), c + 1)
                dve.tensor_copy(xc[:].rearrange("p (h n) -> p h n", h=2), ps[6][:, 0:2, :]).then_inc(sem("E_xc"), 1)
                link(dve.tensor_scalar(pos[:], pos[:], -float(SLOTS), None, ALU.add))
                dve.wait_ge(sem("E_gw"), c + 1)
                link(dve.tensor_copy(wc3[:], ps[7][:, 0, 0:2 * 3 * E8].rearrange("p (h k e) -> p h k e", h=2, k=3)))
                link(dve.tensor_tensor(wc[:], wc3[:, :, 0, :], wc3[:, :, 1, :], ALU.add))
                dve.tensor_tensor(wc[:], wc[:], wc3[:, :, 2, :], ALU.add).then_inc(sem("E_wc"), 1)
                dve.wait_ge(sem("E_wc"), c + 1)
                link(dve.tensor_scalar(wcs[:], wc[:], SELU_SCALE, None, ALU.mult))
                dve.wait_ge(sem("E_wtr"), c + 1)
                dve.tensor_copy(wcT[:], ps[7][0:E8, 1:3, :]).then_inc(sem("E_wcT"), 1)
                dve.wait_ge(sem("E_bias"), c + 1)
                link(dve.tensor_copy(yacc[:], ps[7][:, 0:2, :]))

                def selu(e):
                    dve.wait_ge(sem("E_e"), E8 * c + e + 1)
                    ee, u = act_e[e % 2], act_u[e % 2]
                    link(dve.tensor_scalar(ee[:], ee[:], SELU_ALPHA, -SELU_ALPHA, ALU.min, ALU.add))
                    dve.scalar_tensor_tensor(hid[e % 2][:], u[:], 0.0, ee[:], ALU.max, ALU.add).then_inc(sem("E_hid"), 1)

                def add(e):
                    dve.wait_ge(sem("E_y"), E8 * c + e + 1)
                    for h in range(2):
                        last = dve.scalar_tensor_tensor(yacc[:, h, :], ps[4 + e % 2][:, h, :], wcs[:, h, e:e + 1],
                                                        yacc[:, h, :], ALU.mult, ALU.add)
                    last.then_inc(sem("E_y_out"), 1)
                    dve.wait_ge(sem("E_y_out"), 2 + E8 * c + e + 1)

                for e in range(E8):
                    selu(e)
                    if e >= 1:
                        add(e - 1)
                add(E8 - 1)
                split([y3[:, k, :, :] for k in range(3)], yacc[:], rest[:].rearrange("p (h n) -> p h n", h=2))\
                    .then_inc(sem("E_y3"), 1)
                for q in range(G):
                    dve.wait_ge(sem("E_back"), G * c + q + 1)
                    xt = xs[:, GT * q:GT * (q + 1), :]
                    dve.tensor_tensor(xt, ps[6 + q % 2][:], xt, ALU.add).then_inc(sem("E_x"), 1)
            chain.end(0)


_OUT = (B, P, P)


def kernel(**inputs):
    import numpy as np
    import concourse.bacc as bacc
    from concourse.bass_utils import run_bass_kernel_spmd

    a = {k: np.asarray(w) for k, w in inputs.items()}
    laid = {
        "x": a["x"], "ctxT": a["ctx_768"].reshape(B * P, TD).T,
        "Wq0": a["L0_xattn_Wq"], "bq0": a["L0_xattn_bq"], "Wk0": a["L0_xattn_Wk"], "bk0": a["L0_xattn_bk"],
        "Wv0": a["L0_xattn_Wv"], "bv0": a["L0_xattn_bv"], "Wg": a["L0_ffn_Wg"],
        "W1": a["L0_ffn_W1"].transpose(1, 0, 2).reshape(P, -1),
        "W2": a["L0_ffn_W2"].reshape(E8, F0, P, P).transpose(2, 0, 1, 3).reshape(P, -1),
        "Wq1": a["L1_xattn_Wq"], "Wk1": a["L1_xattn_Wk"], "Wv1": a["L1_xattn_Wv"],
        "Wo1": a["L1_xattn_Wo"].reshape(PAIRS, P, P).transpose(1, 0, 2).reshape(P, -1), "bo1": a["L1_xattn_bo"],
        "gwi": a["L1_ffn_gate_wi"], "gbi": a["L1_ffn_gate_bi"].reshape(F1, P).T,
        "gwo": a["L1_ffn_gate_wo"].reshape(F1, P, P).transpose(1, 0, 2).reshape(P, -1), "gbo": a["L1_ffn_gate_bo"],
        "ewi": a["L1_ffn_exp_wi"].transpose(1, 0, 2).reshape(P, -1),
        "ebi": a["L1_ffn_exp_bi"].reshape(E8 * F1, P).T,
        "ewo": a["L1_ffn_exp_wo"].reshape(E8, F1, P, P).transpose(2, 0, 1, 3).reshape(P, -1),
        "ebo": a["L1_ffn_exp_bo"],
    }
    nc = bacc.Bacc("TRN2", target_bir_lowering=False, num_devices=1)
    arrays, args = {}, []
    for name, w in laid.items():
        w = np.ascontiguousarray(w)
        arrays[f"in_{name}"] = w
        args.append(nc.dram_tensor(f"in_{name}", w.shape, mybir.dt.from_np(w.dtype), kind="ExternalInput").ap())
    args.append(nc.dram_tensor("out_x", _OUT, F32, kind="ExternalOutput").ap())
    build(nc, *args)
    result = run_bass_kernel_spmd(nc, [arrays], core_ids=[0])
    return result.results[0]["out_x"]
```

```python
from contextlib import ExitStack

import concourse.bass as bass
from concourse import mybir

F32 = mybir.dt.float32
F32R = mybir.dt.float32r
BF16 = mybir.dt.bfloat16
I32 = mybir.dt.int32
U32 = mybir.dt.uint32
ALU = mybir.AluOpType
ACT = mybir.ActivationFunctionType
AX = mybir.AxisListType

P = 128
B = 16
TD = 96
GT = 4
G = B // GT
N = GT * P
HEADS, DH = 16, 64
PAIRS = HEADS // 2
E8 = 8
F0 = 256 // P
F1 = 512 // P
EPS = 1e-5
SLOTS = 2 * P
SELU_SCALE = 1.0507009873554805
SELU_ALPHA = 1.6732632423543772
LN_ALPHA = 0.5147757231540873


def stretch(ap, axis, n):
    return ap.broadcast_to([n if k == axis else m for k, m in enumerate(ap.shape)])


def build(nc, x, ctxT, Wq0, bq0, Wk0, bk0, Wv0, bv0, Wg, W1, W2, Wq1, Wk1, Wv1, Wo1, bo1,
          gwi, gbi, gwo, gbo, ewi, ebi, ewo, ebo, out):
    with ExitStack() as stack:
        def sb(name, shape, dt=F32):
            return stack.enter_context(nc.sbuf_tensor(name, shape, dt))

        sems = {}

        def sem(name):
            if name not in sems:
                sems[name] = stack.enter_context(nc.semaphore(name))
            return sems[name]

        def wait(eng, name, n):
            if not isinstance(n, int) or n > 0:
                eng.wait_ge(sem(name), n)

        xs = sb("xs", [P, B, P])
        xT_all = sb("xT_all", [P, B, P])
        wq0, wk0, wv0 = sb("wq0", [P, P]), sb("wk0", [TD, P]), sb("wv0", [TD, P])
        bq0c, bk0c, bv0r = sb("bq0c", [P, 1]), sb("bk0c", [P, 1]), sb("bv0r", [P, P])
        wg = sb("wg", [P, E8])
        w12 = sb("w12", [P, 2, E8, F0, P])
        w1, w2 = w12[:, 0, :, :, :], w12[:, 1, :, :, :]
        xn3 = w12[:].rearrange("p a e f n -> p (a e f n)").bitcast(BF16)[:, 0:3 * B * P]\
            .rearrange("p (k t n) -> p k t n", k=3, t=B)
        w1h, w1l = sb("w1h", [P, E8, F0, P], F32R), sb("w1l", [P, E8, F0, P], F32R)
        xTh, xTl = sb("xTh", [P, GT, P], F32R), sb("xTl", [P, GT, P], F32R)
        wq1, wo1 = sb("wq1", [P, PAIRS, P]), sb("wo1", [P, PAIRS, P])
        wk1, wv1 = sb("wk1", [TD, PAIRS, P]), sb("wv1", [TD, PAIRS, P])
        bo1r = sb("bo1r", [P, P])
        gwis, gwos = sb("gwis", [P, F1, P]), sb("gwos", [P, F1, P])
        gbic, gbor = sb("gbic", [P, F1]), sb("gbor", [P, P])
        ewis, ewos = sb("ewis", [P, E8, F1, P]), sb("ewos", [P, E8, F1, P])
        ebic, ebos = sb("ebic", [P, E8, F1]), sb("ebos", [E8, P])

        ident = sb("ident", [P, P])
        iota = sb("iota", [P, P])
        before = sb("before", [P, P])
        ones = sb("ones", [P, P])
        lnalpha = sb("lnalpha", [P, 1])

        stats, mv = sb("stats", [P, GT, 6]), sb("mv", [P, GT, 2])
        var, rstd = sb("var", [P, GT]), sb("rstd", [P, GT])
        neghalf, carrier = sb("neghalf", [P, GT]), sb("carrier", [P, 1])
        carrier_p = sb("carrier_p", [P, 1])
        ctxg = sb("ctxg", [TD, GT, P])
        xng, xTg = sb("xng", [P, GT, P]), sb("xTg", [P, GT, P])
        vA = sb("vA", [P, GT, P])
        xn = [sb(f"xn{i}", [P, P]) for i in range(2)]
        xnD = [sb(f"xnD{i}", [P, P]) for i in range(2)]
        xT = [sb(f"xT{i}", [P, P]) for i in range(2)]
        ctxb = [sb(f"ctxb{i}", [TD, P]) for i in range(2)]
        ctxh = [sb(f"ctxh{i}", [TD, P], F32R) for i in range(2)]
        ctxl = [sb(f"ctxl{i}", [TD, P], F32R) for i in range(2)]
        wvh, wvl = sb("wvh", [TD, PAIRS, P], F32R), sb("wvl", [TD, PAIRS, P], F32R)
        qk = sb("qk", [P, 4, PAIRS, P])
        qT, kT = [qk[:, i, :, :] for i in range(2)], [qk[:, 2 + i, :, :] for i in range(2)]
        pick = qk[:].rearrange("p a c n -> p (a c n)").bitcast(BF16)[:, 0:B * SLOTS]\
            .rearrange("p (t s) -> p t s", t=B)
        v = [sb(f"v{i}", [P, HEADS, DH]) for i in range(2)]
        shifted = sb("shifted", [P, GT, P])
        pb = sb("pb", [P, 8, GT, P])
        prob, probT = [pb[:, i, :, :] for i in range(4)], [pb[:, 4 + i, :, :] for i in range(4)]
        pickT = pb[:].rearrange("p a c n -> p (a c n)").bitcast(BF16)[:, 0:B * SLOTS]\
            .rearrange("p (t h n) -> p t h n", t=B, h=2)
        smax, ssum = sb("smax", [P, GT]), sb("ssum", [P, GT])
        nmax = [sb(f"nmax{i}", [P, GT]) for i in range(4)]
        psums = [sb(f"psums{i}", [P, GT]) for i in range(4)]
        headsT = sb("headsT", [P, PAIRS, P])
        hid = [sb(f"hid{i}", [P, F1, SLOTS]) for i in range(2)]
        act_u = [qk[:, 2 + i, :, :].rearrange("p c n -> p (c n)").rearrange("p (f s) -> p f s", f=F1) for i in range(2)]
        act_e = [sb(f"act_e{i}", [P, F1, SLOTS]) for i in range(2)]
        hidB = [[hid[k][:, F0 * f:F0 * (f + 1), :].rearrange("p a n -> p (a n)") for f in range(F0)] for k in range(2)]
        hidD = [[h[:, F0 * i:F0 * (i + 1), :].rearrange("p a n -> p (a n)") for h in hid for i in range(2)],
                [pb[:, i, :, :].rearrange("p a n -> p (a n)") for i in range(F1)]]

        top = sb("top", [P, GT, 8])
        topi = sb("topi", [P, GT, 8], U32)
        topf = sb("topf", [P, GT, 8])
        rt1, rt2 = sb("rt1", [P, GT, 8]), sb("rt2", [P, GT, 8])
        rsc = sb("rsc", [P, GT])
        lg = sb("lg", [P, GT, E8])
        glog = [w2[:, E8 - 2 * (2 - i):E8 - 2 * (1 - i), :, :].rearrange("p e f n -> p (e f) n") for i in range(2)]
        w0 = sb("w0", [P, B, E8])
        w_e = sb("w_e", [P, B, E8])

        topD, topiD = sb("topD", [P, B, 8]), sb("topiD", [P, B, 8], U32)
        topfD = sb("topfD", [P, B, 2])
        needed = sb("needed", [P, B])
        gbica = sb("gbica", [P, F1])
        rt16 = sb("rt16", [P, 2, B, E8])
        chosen, sum16 = sb("chosen", [P, B, 2]), sb("sum16", [P, B])
        flag, pos = sb("flag", [P, B]), sb("pos", [P, B])
        rowsum = sb("rowsum", [P, 1])
        ranks = sb("ranks", [P, B])
        nchf, nchi = sb("nchf", [P, 1]), sb("nchi", [P, 1], I32)
        w3 = sb("w3", [P, B, 3, E8], BF16)
        y3 = sb("y3", [P, 3, 2, P], BF16)
        iotab, identb = sb("iotab", [P, SLOTS], BF16), sb("identb", [P, P], BF16)
        xc = sb("xc", [P, SLOTS])
        wc3 = sb("wc3", [P, 2, 3, E8])
        wc, wcs, wcT = sb("wc", [P, 2, E8]), sb("wcs", [P, 2, E8]), sb("wcT", [E8, 2, P])
        yacc = sb("yacc", [P, 2, P])
        rest, rest_p = sb("rest", [P, 2 * P]), sb("rest_p", [P, P])

        ps = [stack.enter_context(nc.psum_tensor(f"ps{i}", [P, GT, P], F32)) for i in range(8)]

        block = stack.enter_context(nc.Block())

        def tile(t, buffer, n=1):
            return buffer[:, t:t + n, :] if isinstance(t, int) else buffer[:, bass.ds(t, n), :]

        def gate_chunk(n):
            g, f = n // F1, (0, 2, 3, 1)[n % F1]
            return g, f, ps[F1 * (g % 2) + f]

        def logits_bank(g, t):
            return gate_chunk(F1 * g + (0 if g == G - 1 and t >= GT // 2 else F1 - 1))[2]

        def chunk_buffer(buffers, n):
            return buffers[n % 2][:, F0 * (n // 2 % 2):F0 * (n // 2 % 2 + 1), :]

        class Chain:
            def __init__(self, eng, name):
                self.eng, self.sem = eng, sem(name)
                self.base, self.n = 0, 0

            def link(self, instruction, carried=False):
                self.n += 1
                instruction.then_inc(self.sem, 1)
                self.eng.wait_ge(self.sem, self.base + self.n)
                if carried and not isinstance(self.base, int):
                    carry_wait(self.eng)

            def loop(self, i, step):
                self.before, self.start = (self.base, self.n), self.n
                self.base = self.base + i * step
                self.step = step

            def end(self, turns):
                assert self.n - self.start == self.step, self.n - self.start
                self.base, self.n = self.before[0] + turns * self.step, self.before[1]

        def carry_wait(eng):
            if eng is nc.vector:
                eng.tensor_copy(carrier[:], neghalf[:, 0:1])
            else:
                eng.tensor_tensor(carrier_p[:], neghalf[:, 0:1], neghalf[:, 0:1], ALU.add)

        @block.sync
        def _(sp):
            def load(dst, src, name):
                sp.dma_start(dst, src).then_inc(sem(name), 16)

            xv = x.rearrange("b p d -> p b d")
            cv = ctxT.rearrange("d (b p) -> d b p", b=B)
            for g in range(G):
                load(xs[:, GT * g:GT * (g + 1), :], xv[:, GT * g:GT * (g + 1), :], f"x_in{g}")
                if g == 0:
                    load(ctxg[:], cv[:, 0:GT, :], "ctxg_in")
                    load(wk0[:], Wk0, "a_in")
                    load(wv0[:], Wv0, "a_in")
                    load(wq0[:], Wq0, "a_in")
                    load(bq0c[:], bq0.rearrange("(p a) -> p a", a=1), "a_in")
                    load(bk0c[:], bk0.rearrange("(p a) -> p a", a=1), "a_in")
                    load(bv0r[:], stretch(bv0.rearrange("(a n) -> a n", a=1), 0, P), "a_in")
            load(wg[:], Wg, "b_in")
            load(w1, W1.rearrange("p (e f n) -> p e f n", e=E8, f=F0), "b_in")
            load(w2, W2.rearrange("p (e f n) -> p e f n", e=E8, f=F0), "b_in")
            load(wq1[:], Wq1.rearrange("p (c n) -> p c n", c=PAIRS), "c_in")
            load(wk1[:], Wk1.rearrange("p (c n) -> p c n", c=PAIRS), "c_in")
            load(wv1[:], Wv1.rearrange("p (c n) -> p c n", c=PAIRS), "c_in")
            load(wo1[:], Wo1.rearrange("p (c n) -> p c n", c=PAIRS), "c_in")
            for b in range(2):
                load(ctxb[b][:], cv[:, b, :], f"ctx_in{b}")
            load(bo1r[:], stretch(bo1.rearrange("(a n) -> a n", a=1), 0, P), "c_in")
            load(gwis[:], gwi.rearrange("p (c n) -> p c n", c=F1), "d_in")
            load(gwos[:], gwo.rearrange("p (c n) -> p c n", c=F1), "d_in")
            load(gbic[:], gbi, "d_in")
            load(gbor[:], stretch(gbo.rearrange("(a n) -> a n", a=1), 0, P), "d_in")
            load(ewis[:], ewi.rearrange("p (e f n) -> p e f n", e=E8, f=F1), "e_in")
            load(ewos[:], ewo.rearrange("p (e f n) -> p e f n", e=E8, f=F1), "e_in")
            load(ebic[:], ebi.rearrange("p (e f) -> p e f", e=E8), "e_in")
            load(ebos[:], ebo, "e_in")
            with sp.Fori(0, G - 1) as g:
                sp.wait_ge(sem("A_v"), g + 1)
                load(ctxg[:], cv[:, bass.ds(GT * g + GT, GT), :], "ctxg_in")
            with sp.Fori(0, B // 2 - 1) as i:
                for par in range(2):
                    sp.wait_ge(sem("C_k1"), 2 * i + par + 1)
                    sp.wait_ge(sem("C_v1"), 2 * i + par + 1)
                    load(ctxb[par][:], cv[:, bass.ds(2 * i + 2 + par, 1), :], f"ctx_in{par}")
            sp.wait_ge(sem("E_count"), 1)
            n_chunks = sp.value_load(nchi[0:1, 0:1], min_val=1, max_val=B // 2)
            ov = out.rearrange("b p d -> p b d")
            for q in range(G):
                sp.wait_ge(sem("E_x"), G * n_chunks + q + 1)
                sp.dma_start(ov[:, GT * q:GT * (q + 1), :], xs[:, GT * q:GT * (q + 1), :]).then_inc(sem("stored"), 16)
            sp.wait_ge(sem("stored"), 16 * G)

        @block.gpsimd
        def _(pool):
            pool.memset(neghalf[:], -0.5).then_inc(sem("filled"), 1)
            pool.memset(var[:], 1.0).then_inc(sem("filled"), 1)
            pool.memset(ones[:], 1.0).then_inc(sem("const"), 1)
            pool.memset(ident[:], 0.0).then_inc(sem("const"), 1)
            pool.memset(lnalpha[:], LN_ALPHA).then_inc(sem("const"), 1)
            pool.iota(iota[:], pattern=[[1, P]], base=0, channel_multiplier=0,
                      allow_small_or_imprecise_dtypes=True).then_inc(sem("const"), 1)
            pool.iota(iotab[:], pattern=[[1, SLOTS]], base=0, channel_multiplier=0,
                      allow_small_or_imprecise_dtypes=True).then_inc(sem("const"), 1)
            pool.wait_ge(sem("const"), 5)
            pool.affine_select(out=ident[:], in_=ident[:], compare_op=ALU.not_equal, fill=1.0, base=0,
                               pattern=[[-1, P]], channel_multiplier=1).then_inc(sem("const"), 1)
            pool.wait_ge(sem("const"), 6)
            pool.tensor_copy(identb[:], ident[:]).then_inc(sem("const"), 1)
            pool.affine_select(out=before[:], in_=ones[:], compare_op=ALU.is_gt, fill=0.0, base=0,
                               pattern=[[1, P]], channel_multiplier=-1).then_inc(sem("const"), 1)

            def power(index):
                pool.wait_ge(sem("ln_var"), index + 1)
                pool.tensor_tensor(rstd[:], var[:], neghalf[:], ALU.pow).then_inc(sem("ln_rstd"), 1)

            pool.wait_ge(sem("filled"), 2)
            for n in range(2):
                power(n)
                half = slice(E8 // 2 * n, E8 // 2 * (n + 1))
                pool.wait_ge(sem("B_w1h"), n + 1)
                pool.tensor_tensor(w1l[:, half, :, :], w1[:, half, :, :], w1h[:, half, :, :].bitcast(F32), ALU.subtract)\
                    .then_inc(sem("B_w1l"), 1)
            with pool.Fori(2, 2 * G) as n:
                power(n)

            def bias(b):
                pool.wait_ge(sem("C_ln"), b + 1)
                pool.tensor_tensor(tile(b, xs), tile(b, xs), bo1r[:].unsqueeze(1), ALU.add)\
                    .then_inc(sem("C_biased"), 1)

            chain = Chain(pool, "pool")

            def keep(d, par, source=xnD):
                pool.wait_ge(sem("C_ln"), d + 5)
                hi, mid, lo = (tile(d, xn3[:, k, :, :]) for k in range(3))
                xd, rp = source[par][:].unsqueeze(1), rest_p[:].unsqueeze(1)
                chain.link(pool.tensor_copy(hi, xd), carried=True)
                chain.link(pool.tensor_tensor(rp, xd, hi, ALU.subtract))
                chain.link(pool.tensor_copy(mid, rp), carried=True)
                chain.link(pool.tensor_tensor(rp, rp, mid, ALU.subtract))
                pool.tensor_copy(lo, rp).then_inc(sem("D_kept"), 1)
                pool.wait_ge(sem("D_kept"), d + 1)

            pool.wait_ge(sem("c_in"), 16 * 5)
            first = 2 * G
            def split_ctx(b, s):
                pool.wait_ge(sem(f"ctx_in{s}"), 8 * (b - s) + 16)
                pool.wait_ge(sem("C_v1"), b - 1)
                carry_wait(pool)
                chain.link(pool.tensor_copy(ctxh[s][:], ctxb[s][:]))
                pool.tensor_tensor(ctxl[s][:], ctxb[s][:], ctxh[s][:].bitcast(F32), ALU.subtract).then_inc(sem("C_ctx"), 1)

            for n in range(4):
                if n == 3:
                    split_ctx(2, 0)
                power(first + n)
                bias(n)
                if n == 0:
                    chain.link(pool.tensor_copy(wvh[:], wv1[:]))
                if n == 1:
                    pool.tensor_tensor(wvl[:], wv1[:], wvh[:].bitcast(F32), ALU.subtract).then_inc(sem("C_wv"), 1)
            with pool.Fori(0, (B - 4) // 2) as i:
                chain.loop(i, 2 * 5)
                for k in range(2):
                    split_ctx(2 * i + 3 + k, 1 - k)
                    power(first + 2 * i + 4 + k)
                    bias(2 * i + 4 + k)
                    keep(2 * i + k, k)
            chain.end((B - 4) // 2)
            split_ctx(B - 1, 1)
            for d in range(B - 4, B):
                power(first + d + 4)
                keep(d, d % 2, xnD if d < B - 1 else xn)
            we, rp = w_e[:], rest_p[:].rearrange("p (t e) -> p t e", e=E8)
            pool.wait_ge(sem("D_weights"), 1)
            pool.wait_ge(sem("D_places"), 1)
            for k in range(2):
                last = pool.tensor_tensor(rt16[:, k, :, :], rt16[:, k, :, :], stretch(topD[:, :, k:k + 1], 2, E8), ALU.mult)
            chain.link(last)
            chain.link(pool.tensor_tensor(we, rt16[:, 0, :, :], rt16[:, 1, :, :], ALU.add))
            chain.link(pool.tensor_copy(w3[:, :, 0, :], we))
            chain.link(pool.tensor_tensor(rp, we, w3[:, :, 0, :], ALU.subtract))
            chain.link(pool.tensor_copy(w3[:, :, 1, :], rp))
            chain.link(pool.tensor_tensor(rp, rp, w3[:, :, 1, :], ALU.subtract))
            pool.tensor_copy(w3[:, :, 2, :], rp).then_inc(sem("E_w3"), 1)

        CONST = 8

        @block.tensor
        def _(pe):
            def mm(dst, lhsT, rhs, start=True, stop=True):
                return pe.matmul(dst, lhsT, rhs, start=start, stop=stop)

            def mm_parts(bank, stationary, moving):
                (sh, sl), (mh, ml) = stationary, moving
                mm(bank[:], sh, mh, stop=False)
                mm(bank[:], sh, ml, start=False, stop=False)
                return mm(bank[:], sl, mh, start=False)

            pe.sem_inc(sem("B_y"), 2)
            pe.wait_ge(sem("const"), CONST)
            def a_project_k(n):
                pe.wait_ge(sem("A_ln"), n + 1)
                wait(pe, "B_lshift", n)
                for t in range(GT):
                    last = pe.transpose(ps[6][:, t, :], xng[:, t, :], ident[:])
                last.then_inc(sem("A_tr"), 1)
                pe.wait_ge(sem("ctxg_in"), 16 * n + 16)
                wait(pe, "B_xTh", n)
                mm(ps[7][:], wk0[:], ctxg[:]).then_inc(sem("A_k"), 1)

            def a_project_qv(n):
                pe.wait_ge(sem("A_xT"), n + 1)
                mm(ps[6][:], wq0[:], xTg[:]).then_inc(sem("A_q"), 1)
                pe.wait_ge(sem("A_k_out"), n + 1)
                for t in range(GT):
                    last = mm(ps[7][:, t, :], ctxg[:, t, :], wv0[:])
                last.then_inc(sem("A_v"), 1)

            def a_scores(n):
                pe.wait_ge(sem("A_q_out"), n + 1)
                for t in range(GT):
                    last = mm(ps[6][:, t, :], qT[1][:, t, :], kT[1][:, t, :])
                last.then_inc(sem("A_s"), 1)

            def a_transpose(n):
                pe.wait_ge(sem("A_exp"), n + 1)
                pe.wait_ge(sem("A_v_out"), n + 1)
                for t in range(GT):
                    last = pe.transpose(ps[7][:, t, :], prob[0][:, t, :], ident[:])
                last.then_inc(sem("A_ptr"), 1)

            def a_attend(n):
                pe.wait_ge(sem("A_pT"), n + 1)
                for t in range(GT):
                    last = mm(ps[6][:, t, :], probT[0][:, t, :], vA[:, t, :])
                last.then_inc(sem("A_o"), 1)

            def b_transpose(n):
                pe.wait_ge(sem("B_ln"), n + 1)
                for t in range(GT):
                    last = pe.transpose(ps[7][:, t, :], xng[:, t, :], ident[:])
                last.then_inc(sem("B_tr"), 1)

            def b_logits(n):
                pe.wait_ge(sem("B_xT"), n + 1)
                for t in range(GT):
                    last = mm(ps[6][:, t, 0:E8], xTg[:, t, :], wg[:])
                last.then_inc(sem("B_l"), 1)

            def hidden(g, e):
                if e == 0:
                    pe.wait_ge(sem("B_xTl"), g + 1)
                pe.wait_ge(sem("B_relu"), E8 * g + e + 1)
                for f in range(F0):
                    bank = ps[F0 * (e % 2) + f]
                    mm_parts(bank, (w1h[:, e, f, :], w1l[:, e, f, :]), (xTh[:], xTl[:])).then_inc(sem("B_h"), 1)

            def output(g, e):
                pe.wait_ge(sem("B_relu"), 2 + E8 * g + e + 1)
                pe.wait_ge(sem("B_y_out"), E8 * g + e + 1)
                for t in range(GT):
                    for f in range(F0):
                        last = mm(ps[4 + e % 2][:, t, :], hidB[e % 2][f][:, P * t:P * t + P], w2[:, e, f, :],
                                  start=f == 0, stop=f == F0 - 1)
                last.then_inc(sem("B_y"), 1)

            def experts(g, n=None):
                steps = {0: a_project_k, 1: a_project_qv, 2: a_scores, 3: a_transpose, 4: a_attend, 6: b_transpose}
                b_logits(g)
                hidden(g, 0)
                for e in range(E8):
                    if n is None and e == E8 - 2:
                        pe.wait_ge(sem("B_relu"), 2 + E8 * g + e + 1)
                        transpose_x(0, 0, d=False)
                    if e + 1 < E8:
                        hidden(g, e + 1)
                    if n is None and e == E8 - 1:
                        project_q(0, 0)
                    output(g, e)
                    if n is not None and e in steps:
                        steps[e](n)

            pe.wait_ge(sem("a_in"), 16 * 6)
            for step in (a_project_k, a_project_qv, a_scores, a_transpose, a_attend):
                step(0)
            pe.wait_ge(sem("c_in"), 16 * 5)
            pe.wait_ge(sem("ctx_in0"), 16)
            for c in range(2):
                for i in range(GT):
                    last = mm(ps[c][:, i, :], wk1[:, GT * c + i, :], ctxb[0][:])
                last.then_inc(sem(f"C_k{c}"), 1)
            for c in range(2):
                mm(ps[2 + c][:], ctxb[0][:], wv1[:, GT * c:GT * (c + 1), :]).then_inc(sem(f"C_v{c}"), 1)
            b_transpose(0)
            pe.wait_ge(sem("b_in"), 16 * 3)
            pe.wait_ge(sem("B_w1l"), 2)
            for name in ("C_k0_out", "C_k1_out", "C_v0_out", "C_v1_out"):
                pe.wait_ge(sem(name), 1)
            with pe.Fori(0, G - 1) as g:
                experts(g, g + 1)

            def gate_hidden(n):
                g, f, bank = gate_chunk(n)
                if n == 0:
                    pe.wait_ge(sem("d_in"), 16 * 4)
                wait(pe, "D_u", n - 2 * F1 + 1)
                if f == 1:
                    wait(pe, "D_glog", g - 1)
                mm(bank[:], gwis[:, f, :], xT_all[:, GT * g:GT * (g + 1), :]).then_inc(sem("D_h"), 1)

            def transposes_p(b, u):
                for a in range(2):
                    pe.wait_ge(sem(f"C_prob{u}{a}"), b + 1)
                    wait(pe, f"C_pT{1 - u}{a}", b if u == 0 else b + 1)
                    for h in range(GT):
                        last = pe.transpose(ps[4 + a][:, h, :], prob[2 * u + a][:, h, :], ident[:])
                    last.then_inc(sem(f"C_ptr{u}{a}"), 1)

            def attend(b, s, u):
                if u == 0:
                    pe.wait_ge(sem("C_v0_out"), b + 1)
                    pe.wait_ge(sem("C_v1_out"), b + 1)
                wait(pe, f"C_hT{u}", b)
                for a in range(2):
                    pe.wait_ge(sem(f"C_pT{u}{a}"), b + 1)
                for h in range(GT):
                    for a in range(2):
                        last = mm(ps[6 + u][DH * a:DH * (a + 1), h, :], v[s][:, 2 * GT * u + 2 * h + a, :],
                                  probT[2 * u + a][:, h, :])
                last.then_inc(sem(f"C_o{u}"), 1)

            def scores(b, s, u):
                if u == 0:
                    for name in ("C_q0_out", "C_q1_out", "C_k0_out", "C_k1_out"):
                        pe.wait_ge(sem(name), b + 1)
                for a in range(2):
                    wait(pe, f"C_exp{1 - u}{a}", b if u == 0 else b + 1)
                for h in range(GT):
                    for a in range(2):
                        last = mm(ps[2 + a][:, h, :], qT[s][DH * a:DH * (a + 1), GT * u + h, :],
                                  kT[s][DH * a:DH * (a + 1), GT * u + h, :])
                last.then_inc(sem(f"C_s{u}"), 1)

            def transpose_x(b, s, d=True, x=True):
                pe.wait_ge(sem("C_ln"), b + 1)
                wait(pe, "C_v0_out", b if x else B)
                if isinstance(b, int) and b == 1:
                    pe.wait_ge(sem("C_q1_out"), 1)
                if isinstance(b, int) and b == 2:
                    pe.wait_ge(sem("C_k0_out"), 2)
                if not x:
                    wait(pe, "C_xT", b)
                if d:
                    last = pe.transpose(ps[0][:, 1, :], xnD[s][:], ident[:])
                if x:
                    last = pe.transpose(ps[0][:, 0, :], xn[s][:], ident[:])
                last.then_inc(sem("C_xtr"), 1)

            def project_q(b, s):
                pe.wait_ge(sem("C_xT"), b + 1)
                wait(pe, "C_v1_out", b)
                for c, bank in ((0, 1), (1, 0)):
                    for i in range(GT):
                        last = mm(ps[bank][:, i, :], wq1[:, GT * c + i, :], xT[s][:])
                    last.then_inc(sem(f"C_q{c}"), 1)

            def project_k(b, s, n_ctx, after_out):
                pe.wait_ge(sem(f"ctx_in{s}"), n_ctx)
                for c in range(2):
                    bank = c
                    pe.wait_ge(sem(f"C_q{1 - c}_out"), b + 1)
                    if c == 1:
                        wait(pe, "C_x", after_out)
                    for i in range(GT):
                        last = mm(ps[bank][:, i, :], wk1[:, GT * c + i, :], ctxb[s][:])
                    last.then_inc(sem(f"C_k{c}"), 1)

            def project_v_early(b, bank):
                for c in range(2):
                    mm(ps[bank + c][:], ctxb[b][:], wv1[:, GT * c:GT * (c + 1), :]).then_inc(sem(f"C_v{c}"), 1)

            def project_v(b, s):
                for c in range(2):
                    pe.wait_ge(sem(f"C_k{c}_out"), b + 1)
                    pe.wait_ge(sem("C_wv"), 1)
                    pe.wait_ge(sem("C_ctx"), b - 1)
                    some = slice(GT * c, GT * (c + 1))
                    mm_parts(ps[c], (ctxh[s][:], ctxl[s][:]), (wvh[:, some, :], wvl[:, some, :]))\
                        .then_inc(sem(f"C_v{c}"), 1)

            def project_out(b, has_next):
                pe.wait_ge(sem("C_hT0"), b + 1)
                pe.wait_ge(sem("C_hT1"), b + 1)
                if has_next:
                    pe.wait_ge(sem("C_q0_out"), b + 3)
                else:
                    pe.wait_ge(sem("C_v1_out"), B)
                    wait(pe, "C_x", b)
                for c in range(PAIRS):
                    last = mm(ps[1][:, 0, :], headsT[:, c, :], wo1[:, c, :], start=c == 0, stop=c == PAIRS - 1)
                last.then_inc(sem("C_out"), 1)

            def body(b, s, n_ctx, first=False, last=False):
                transpose_x(b + 1, 1 - s, d=not isinstance(b, int) or b >= 3, x=not last)
                scores(b, s, 0)
                if not first:
                    transposes_p(b - 1, 1)
                if not last:
                    project_q(b + 1, 1 - s)
                else:
                    pe.wait_ge(sem("C_xT"), B + 1)
                    gate_hidden(0)
                if not first:
                    attend(b - 1, 1 - s, 1)
                else:
                    pe.wait_ge(sem("ctx_in1"), 16)
                    project_v_early(b + 1, bank=6)
                    pe.wait_ge(sem("B_y_out"), 2 + E8 * G)
                scores(b, s, 1)
                transposes_p(b, 0)
                if not first:
                    project_out(b - 1, not last)
                else:
                    project_k(b + 1, 1 - s, n_ctx, b)
                    for c in range(2):
                        pe.wait_ge(sem(f"C_v{c}_out"), b + 2)
                attend(b, s, 0)
                if not first and not last:
                    project_k(b + 1, 1 - s, n_ctx, b)
                    project_v(b + 1, 1 - s)

            experts(G - 1)
            for b in range(4):
                body(b, b % 2, 16 * (1 + (b + 1) // 2) , first=b == 0)
            with pe.Fori(0, B // 2 - 3) as i:
                body(2 * i + 4, 0, 16 * i + 48)
                body(2 * i + 5, 1, 16 * i + 64)
            body(B - 2, 0, 16 * (B // 2))
            body(B - 1, 1, None, last=True)
            pe.wait_ge(sem("C_exp10"), B)
            gate_hidden(1)
            transposes_p(B - 1, 1)
            pe.wait_ge(sem("C_exp11"), B)
            gate_hidden(2)
            attend(B - 1, 1, 1)
            project_out(B - 1, False)
            pe.wait_ge(sem("C_x"), B)
            gate_hidden(3)
            for name in ("C_pT10", "C_pT11", "C_hT0", "C_hT1"):
                pe.wait_ge(sem(name), B)

            for g in range(G):
                if g + 1 == G - 1:
                    pe.wait_ge(sem("C_ln"), B + 4)
                    pe.wait_ge(sem("D_u"), F1 + 1)
                    for i, source in enumerate((xnD[1], xnD[0], xn[1])):
                        last = pe.transpose(ps[F1][:, i, :], source[:], ident[:])
                    last.then_inc(sem("C_xtr"), 1)
                    pe.wait_ge(sem("C_xT"), B + 2)
                if g + 1 < G:
                    for n in range(F1 * (g + 1), F1 * (g + 2)):
                        gate_hidden(n)
                pe.wait_ge(sem("D_selu"), F1 * (g + 1))
                for t in range(GT):
                    for f in range(F1):
                        last = mm(logits_bank(g, t)[:, t, :], hidD[g % 2][f][:, P * t:P * t + P],
                                  gwos[:, f, :], start=f == 0, stop=f == F1 - 1)
                    if t % 2 == 1:
                        last.then_inc(sem("D_l"), 1)

            pe.wait_ge(sem("E_rowsum"), 1)
            mm(ps[5][:, 0, 0:1], before[:], rowsum[:])
            mm(ps[5][:, 1, 0:1], ones[:], rowsum[:]).then_inc(sem("E_ranked"), 1)
            pe.wait_ge(sem("e_in"), 16 * 4)
            pe.wait_ge(sem("D_kept"), B)
            pe.wait_ge(sem("E_count"), 1)
            n_chunks = pe.value_load(nchi[0:1, 0:1], min_val=1, max_val=B // 2)
            xcb, wcb = ps[6][:, 0:2, :], ps[7][:, 0, 0:2 * 3 * E8].rearrange("p (h k) -> p h k", h=2)

            def transpose_pick(c, q):
                pe.wait_ge(sem("E_xc"), c + 1)
                if q > 0:
                    pe.wait_ge(sem("E_pickT"), G * c + q)
                bank = ps[6][:].rearrange("p t n -> p (t n)").bitcast(BF16).rearrange("p (t h n) -> p t h n", t=GT, h=2)
                for t in range(GT):
                    for h in range(2):
                        last = pe.transpose(bank[:, t, h, :], pick[:, GT * q + t, P * h:P * h + P], identb[:])
                last.then_inc(sem("E_ptr"), 1)

            with pe.Fori(0, n_chunks) as c:
                pe.wait_ge(sem("E_x"), G * (c + 1))
                for t in range(B):
                    if t % GT == 0:
                        pe.wait_ge(sem("E_pick"), G * c + t // GT + 1)
                    for k in range(3):
                        last = mm(xcb, xn3[:, k, t, :], pick[:, t, :], start=t == 0 and k == 0, stop=t == B - 1 and k == 2)
                last.then_inc(sem("E_gx"), 1)

                def hidden(e):
                    for i in range(2):
                        pe.wait_ge(sem("E_u"), 2 * (E8 * c + e) + i + 1)
                        for f in range(2):
                            last = mm(ps[2 * (e % 2) + i][:, 2 * f:2 * f + 2, :], ewis[:, e, 2 * i + f, :], xc[:])
                        last.then_inc(sem("E_h"), 1)

                def output(e):
                    pe.wait_ge(sem("E_hid"), 4 + 2 * (E8 * c + e + 1))
                    pe.wait_ge(sem("E_y_out"), E8 * c + e + 1)
                    for h in range(2):
                        for f in range(F1):
                            last = mm(ps[4 + e % 2][:, h, :], hid[e % 2][:, f, P * h:P * h + P], ewos[:, e, f, :],
                                      start=f == 0, stop=f == F1 - 1)
                    last.then_inc(sem("E_y"), 1)

                pe.wait_ge(sem("E_xc"), c + 1)
                hidden(0)
                pe.wait_ge(sem("E_w3"), 1)
                for h in range(2):
                    for t in range(B):
                        last = mm(wcb[:, h, :], pick[:, t, P * h:P * h + P], w3[:, t, :, :], start=t == 0, stop=t == B - 1)
                last.then_inc(sem("E_gw"), 1)
                hidden(1)
                pe.wait_ge(sem("E_wc"), c + 1)
                for h in range(2):
                    last = pe.transpose(ps[7][0:E8, 1 + h, :], wc[:, h, :], ident[:])
                last.then_inc(sem("E_wtr"), 1)
                transpose_pick(c, 0)
                for e in range(2, E8):
                    hidden(e)
                    if e == 2:
                        pe.wait_ge(sem("E_wcT"), c + 1)
                        for h in range(2):
                            last = mm(ps[7][:, h, :], wcT[:, h, :], ebos[:])
                        last.then_inc(sem("E_bias"), 1)
                    output(e - 2)
                    if e % 2 == 0:
                        transpose_pick(c, e // 2)
                output(E8 - 2)
                output(E8 - 1)
                pe.wait_ge(sem("E_y3"), c + 1)
                pe.wait_ge(sem("E_pickT"), G * (c + 1))
                for q in range(G):
                    pe.wait_ge(sem("E_x"), G * c + q + 3)
                    for t in range(GT):
                        for h in range(2):
                            for k in range(3):
                                last = mm(ps[6 + q % 2][:, t, :], pickT[:, GT * q + t, h, :], y3[:, k, h, :],
                                          start=h == 0 and k == 0, stop=h == 1 and k == 2)
                    last.then_inc(sem("E_back"), 1)

        @block.scalar
        def _(act):
            for name, n in (("B_relu", 2), ("E_u", 4)):
                act.sem_inc(sem(name), n)

            def a_project_k(n):
                act.wait_ge(sem("A_tr"), n + 1)
                act.copy(xTg[:], ps[6][:]).then_inc(sem("A_xT"), 1)
                act.wait_ge(sem("A_k"), n + 1)
                act.activation(kT[1][:, 0:GT, :], ps[7][:], ACT.Identity, bias=bk0c[:]).then_inc(sem("A_k_out"), 1)

            def a_project_q(n):
                act.wait_ge(sem("A_q"), n + 1)
                act.activation(qT[1][:, 0:GT, :], ps[6][:], ACT.Identity, bias=bq0c[:]).then_inc(sem("A_q_out"), 1)

            def a_exp(n):
                act.wait_ge(sem("A_shift"), n + 1)
                act.activation(prob[0][:], shifted[:], ACT.Exp, scale=P ** -0.5).then_inc(sem("A_exp"), 1)

            def a_copy_pT(n):
                act.wait_ge(sem("A_ptr"), n + 1)
                act.copy(probT[0][:], ps[7][:]).then_inc(sem("A_pT"), 1)

            def b_copy_xT(n):
                act.wait_ge(sem("B_tr"), n + 1)
                act.copy(xTg[:], ps[7][:]).then_inc(sem("B_xT"), 1)
                act.copy(xTh[:], ps[7][:]).then_inc(sem("B_xTh"), 1)

            def b_exp(n):
                act.wait_ge(sem("B_lshift"), n + 1)
                act.activation(lg[:], rt1[:], ACT.Exp).then_inc(sem("B_lexp"), 1)

            def relu(g, e):
                act.wait_ge(sem("B_y"), E8 * g + e + 1)
                for f in range(F0):
                    act.wait_ge(sem("B_h"), F0 * (E8 * g + e) + f + 1)
                    last = act.activation(hidB[e % 2][f], ps[F0 * (e % 2) + f][:].rearrange("p t n -> p (t n)"), ACT.Relu)
                last.then_inc(sem("B_relu"), 1)

            def experts(g, n=None):
                steps = {1: a_project_k, 2: a_project_q, 3: a_exp, 4: a_copy_pT, 7: b_copy_xT}
                for e in range(E8):
                    relu(g, e)
                    if n is None and e == E8 - 2:
                        copy_x(0, 0, d=False)
                    if e == 1:
                        b_exp(g)
                    if n is not None and e in steps:
                        steps[e](n)

            act.wait_ge(sem("a_in"), 16 * 6)
            for step in (a_project_k, a_project_q, a_exp):
                step(0)
            act.wait_ge(sem("b_in"), 16 * 3)
            act.copy(w1h[:, 0:E8 // 2, :, :], w1[:, 0:E8 // 2, :, :]).then_inc(sem("B_w1h"), 1)
            a_copy_pT(0)
            act.copy(w1h[:, E8 // 2:E8, :, :], w1[:, E8 // 2:E8, :, :]).then_inc(sem("B_w1h"), 1)
            for c in range(2):
                act.wait_ge(sem(f"C_k{c}"), 1)
                act.copy(kT[0][:, GT * c:GT * (c + 1), :], ps[c][:]).then_inc(sem(f"C_k{c}_out"), 1)
            for c in range(2):
                act.wait_ge(sem(f"C_v{c}"), 1)
                act.copy(v[0][:, 8 * c:8 * (c + 1), :], ps[2 + c][:].rearrange("p t (h d) -> p (t h) d", d=DH))\
                    .then_inc(sem(f"C_v{c}_out"), 1)
            b_copy_xT(0)
            with act.Fori(0, G - 1) as g:
                experts(g, g + 1)

            def copy_pT(b, u):
                for a in range(2 - u):
                    act.wait_ge(sem(f"C_ptr{u}{a}"), b + 1)
                    wait(act, f"C_o{u}", b)
                    act.copy(probT[2 * u + a][:], ps[4 + a][:]).then_inc(sem(f"C_pT{u}{a}"), 1)

            def exp(b, u):
                for a in range(2):
                    act.wait_ge(sem(f"C_max{u}{a}"), b + 1)
                    wait(act, f"C_ptr{u}{a}", b)
                    for h in range(GT):
                        last = act.activation(prob[2 * u + a][:, h, :], ps[2 + a][:, h, :], ACT.Exp,
                                              bias=nmax[2 * u + a][:, h:h + 1],
                                              accum_out=psums[2 * u + a][:, h:h + 1] if a == 1 else None)
                    last.then_inc(sem(f"C_exp{u}{a}"), 1)

            def copy_x(b, s, d=True, x=True):
                act.wait_ge(sem("C_xtr"), b + 1)
                if d:
                    last = act.copy(tile(b - 4, xT_all), ps[0][:, 1:2, :])
                if x:
                    wait(act, "C_q1", b - 1)
                    last = act.copy(xT[s][:], ps[0][:, 0, :])
                last.then_inc(sem("C_xT"), 1)

            def copy_q(b, s):
                for c, bank in ((0, 1), (1, 0)):
                    act.wait_ge(sem(f"C_q{c}"), b + 1)
                    wait(act, "C_s1", b - 1)
                    act.activation(qT[s][:, GT * c:GT * (c + 1), :], ps[bank][:], ACT.Identity, scale=DH ** -0.5).then_inc(sem(f"C_q{c}_out"), 1)

            def copy_k(b, s):
                act.wait_ge(sem("C_k0"), b + 1)
                wait(act, "C_s1", b - 1)
                act.copy(kT[s][:, 0:GT, :], ps[0][:]).then_inc(sem("C_k0_out"), 1)

            def copy_v(b, s, bank=0):
                act.wait_ge(sem("C_v0"), b + 1)
                wait(act, "C_o1", b - 1)
                act.copy(v[s][:, 0:8, :], ps[bank][:].rearrange("p t (h d) -> p (t h) d", d=DH)).then_inc(sem("C_v0_out"), 1)

            def copy_heads(b, u):
                act.wait_ge(sem(f"C_o{u}"), b + 1)
                wait(act, "C_out", b)
                act.copy(headsT[:, GT * u:GT * (u + 1), :], ps[6 + u][:]).then_inc(sem(f"C_hT{u}"), 1)

            def body(b, s, first=False, last=False):
                copy_x(b + 1, 1 - s, d=not isinstance(b, int) or b >= 3, x=not last)
                if not first:
                    copy_pT(b - 1, 1)
                exp(b, 0)
                if not first:
                    copy_heads(b - 1, 1)
                if not last:
                    copy_q(b + 1, 1 - s)
                if first:
                    copy_v(b + 1, 1 - s, bank=6)
                copy_pT(b, 0)
                if first:
                    copy_k(b + 1, 1 - s)
                exp(b, 1)
                if not first and not last:
                    copy_k(b + 1, 1 - s)
                copy_heads(b, 0)
                if not first and not last:
                    copy_v(b + 1, 1 - s)

            experts(G - 1)
            copy_q(0, 0)
            for b in range(4):
                body(b, b % 2, first=b == 0)
            with act.Fori(0, B // 2 - 3) as i:
                body(2 * i + 4, 0)
                body(2 * i + 5, 1)
            body(B - 2, 0)
            body(B - 1, 1, last=True)

            def gate_hidden(n):
                g, f, bank = gate_chunk(n)
                act.wait_ge(sem("D_h"), n + 1)
                wait(act, "D_selu", n - 3)
                bank = bank[:].rearrange("p (a t) n -> p a (t n)", a=2)
                act.activation(chunk_buffer(act_e, n), bank, ACT.Exp, bias=gbica[:, f:f + 1]).then_inc(sem("D_exp"), 1)
                act.activation(chunk_buffer(act_u, n), bank, ACT.Identity, bias=gbic[:, f:f + 1]).then_inc(sem("D_u"), 1)

            act.wait_ge(sem("D_bias"), 1)
            gate_hidden(0)
            copy_pT(B - 1, 1)
            gate_hidden(1)
            copy_heads(B - 1, 1)
            for n in range(2, F1 * G):
                if n == F1 * (G - 1):
                    act.wait_ge(sem("C_xtr"), B + 2)
                    act.copy(xT_all[:, B - 3:B, :], ps[F1][:, 0:3, :]).then_inc(sem("C_xT"), 1)
                gate_hidden(n)

            act.wait_ge(sem("E_count"), 1)
            n_chunks = act.value_load(nchi[0:1, 0:1], min_val=1, max_val=B // 2)
            with act.Fori(0, n_chunks) as c:
                def hidden(e):
                    for i in range(2):
                        n = 2 * (E8 * c + e) + i + 1
                        act.wait_ge(sem("E_h"), n)
                        act.wait_ge(sem("E_hid"), n)
                        for f in (2 * i, 2 * i + 1):
                            last = act.activation(act_u[e % 2][:, f, :], ps[2 * (e % 2) + i][:, 2 * (f % 2):2 * (f % 2) + 2, :],
                                                  ACT.Identity, bias=ebic[:, e, f:f + 1])
                        last.then_inc(sem("E_u"), 1)
                        act.wait_ge(sem("E_u"), 4 + n)
                        act.activation(act_e[e % 2][:, 2 * i:2 * i + 2, :], act_u[e % 2][:, 2 * i:2 * i + 2, :],
                                       ACT.Exp, bias=lnalpha[:]).then_inc(sem("E_e"), 1)

                def copy_pick(q):
                    act.wait_ge(sem("E_ptr"), G * c + q + 1)
                    bank = ps[6][:].rearrange("p t n -> p (t n)").bitcast(BF16).rearrange("p (t h n) -> p t h n", t=GT, h=2)
                    act.copy(pickT[:, GT * q:GT * (q + 1), :, :], bank).then_inc(sem("E_pickT"), 1)

                for e in range(E8):
                    hidden(e)
                    if e % 2 == 1:
                        copy_pick(e // 2)

        @block.vector
        def _(dve):
            chain = Chain(dve, "dve")
            link = chain.link

            def layer_norm(tiles, done, index):
                if not isinstance(index, int):
                    carry_wait(dve)
                for t, (src, _) in enumerate(tiles):
                    last = dve.bn_stats(stats[:, t, :], src)
                link(last, carried=True)
                for t in range(len(tiles)):
                    last = dve.bn_aggr(mv[:, t, :], stats[:, t, :])
                link(last)
                dve.tensor_scalar(var[:, 0:len(tiles)], mv[:, 0:len(tiles), 1], EPS, None, ALU.add).then_inc(sem("ln_var"), 1)
                dve.wait_ge(sem("ln_rstd"), index + 1)
                for t, (src, dst) in enumerate(tiles):
                    last = dve.tensor_scalar(dst, src, mv[:, t, 0:1], rstd[:, t:t + 1], ALU.subtract, ALU.mult)
                last.then_inc(sem(done), 1)

            def find_top(values, v=top, i=topi, n=GT):
                for t in range(n):
                    last = dve.max(v[:, t, :], values(t))
                link(last, carried=True)
                for t in range(n):
                    last = dve.max_index(i[:, t, :], v[:, t, :], values(t))
                link(last)

            def place(value, index, r1, r2, r3, n, dst):
                link(dve.tensor_tensor(r3.unsqueeze(2), value[:, :, 0:1], value[:, :, 1:2], ALU.add))
                link(dve.reciprocal(r3, r3))
                link(dve.tensor_tensor(value[:, :, 0:2], value[:, :, 0:2], stretch(r3.unsqueeze(2), 2, 2), ALU.mult))
                eight = stretch(iota[:, 0:E8].unsqueeze(1), 1, n)
                for k, r in ((0, r1), (1, r2)):
                    last = dve.tensor_tensor(r, eight, stretch(index[:, :, k:k + 1], 2, E8), ALU.is_equal)
                link(last)
                for k, r in ((0, r1), (1, r2)):
                    last = dve.tensor_tensor(r, r, stretch(value[:, :, k:k + 1], 2, E8), ALU.mult)
                link(last)
                return dve.tensor_tensor(dst, r1, r2, ALU.add)

            for name, n in (("B_y_out", 2), ("E_hid", 4), ("E_y_out", 2), ("E_x", G)):
                dve.sem_inc(sem(name), n)
            dve.wait_ge(sem("filled"), 2)

            def group(n):
                return [(tile(GT * n + t, xs), xng[:, t:t + 1, :]) for t in range(GT)]

            def a_norm(n):
                wait(dve, "B_tr", n)
                layer_norm(group(n), "A_ln", 2 * n)

            def a_copy_v(n):
                dve.wait_ge(sem("A_v"), n + 1)
                dve.tensor_tensor(vA[:], ps[7][:], stretch(bv0r[:].unsqueeze(1), 1, GT), ALU.add)\
                    .then_inc(sem("A_v_out"), 1)

            def a_shift(n):
                dve.wait_ge(sem("A_s"), n + 1)
                link(dve.tensor_reduce(smax[:], ps[6][:], AX.X, ALU.max))
                dve.tensor_tensor(shifted[:], ps[6][:], stretch(smax[:].unsqueeze(2), 2, P), ALU.subtract)\
                    .then_inc(sem("A_shift"), 1)

            def a_sum(n):
                dve.wait_ge(sem("A_exp"), n + 1)
                link(dve.tensor_reduce(ssum[:], prob[0][:], AX.X, ALU.add))
                link(dve.reciprocal(ssum[:], ssum[:]))

            def a_add(n):
                dve.wait_ge(sem("A_o"), n + 1)
                for t in range(GT):
                    xt = tile(GT * n + t, xs)
                    last = dve.scalar_tensor_tensor(xt, ps[6][:, t:t + 1, :], ssum[:, t:t + 1], xt, ALU.mult, ALU.add)
                last.then_inc(sem("A_x"), 1)
                dve.wait_ge(sem("A_x"), n + 1)
                layer_norm(group(n), "B_ln", 2 * n + 1)

            def b_shift(n):
                dve.wait_ge(sem("B_l"), n + 1)
                bank = ps[6][:, :, 0:E8]
                link(dve.tensor_reduce(smax[:], bank, AX.X, ALU.max))
                dve.tensor_tensor(rt1[:], bank, stretch(smax[:].unsqueeze(2), 2, E8), ALU.subtract)\
                    .then_inc(sem("B_lshift"), 1)

            def b_route(n):
                dve.wait_ge(sem("B_lexp"), n + 1)
                link(dve.tensor_reduce(rsc[:], lg[:], AX.X, ALU.add))
                link(dve.reciprocal(rsc[:], rsc[:]))
                link(dve.tensor_tensor(lg[:], lg[:], stretch(rsc[:].unsqueeze(2), 2, E8), ALU.mult), carried=True)
                find_top(lambda t: lg[:, t, :])
                link(dve.tensor_copy(topf[:], topi[:]))
                link(place(top, topf, rt1[:], rt2[:], rsc[:], GT, tile(GT * n, w0, GT)))

            def b_split_xT(n):
                dve.wait_ge(sem("B_xTh"), n + 1)
                dve.tensor_tensor(xTl[:], xTg[:], xTh[:].bitcast(F32), ALU.subtract).then_inc(sem("B_xTl"), 1)

            def experts(g, n=None):
                steps = {1: a_copy_v, 2: a_shift, 3: a_sum, 4: a_add}
                b_shift(g)
                if n is not None:
                    a_norm(n)
                b_route(g)
                for e in range(E8):
                    if n is not None and e == E8 - 1:
                        b_split_xT(n)
                    dve.wait_ge(sem("B_y"), 2 + E8 * g + e + 1)
                    for t in range(GT):
                        xt = tile(GT * g + t, xs)
                        last = dve.scalar_tensor_tensor(xt, ps[4 + e % 2][:, t:t + 1, :], tile(GT * g + t, w0)[:, 0, e:e + 1],
                                                        xt, ALU.mult, ALU.add)
                    last.then_inc(sem("B_y_out"), 1)
                    dve.wait_ge(sem("B_y_out"), 2 + E8 * g + e + 1)
                    if n is not None and e in steps:
                        steps[e](n)
                    if n is None and e in (1, 3):
                        b = e // 2
                        layer_norm([(tile(b, xs), xn[b][:].unsqueeze(1))], "C_ln", 2 * G + b)

            dve.wait_ge(sem("x_in0"), 16)
            a_norm(0)
            dve.wait_ge(sem("a_in"), 16 * 6)
            for step in (a_copy_v, a_shift, a_sum, a_add, b_split_xT):
                step(0)
            for g in range(1, G):
                dve.wait_ge(sem(f"x_in{g}"), 16)
            with dve.Fori(0, G - 1) as g:
                chain.loop(g, 20)
                experts(g, g + 1)
            chain.end(G - 1)
            dve.wait_ge(sem("const"), CONST)

            def norm(b, s, c=True, d=True):
                tiles = []
                if d:
                    wait(dve, "D_kept", b - 3)
                    tiles.append((tile(b - 2, xs), xnD[s][:].unsqueeze(1)))
                if c:
                    tiles.append((tile(b + 2, xs), xn[s][:].unsqueeze(1)))
                wait(dve, "C_xtr", b + 1)
                layer_norm(tiles, "C_ln", 2 * G + b + 2)

            def peak(b, u):
                dve.wait_ge(sem(f"C_s{u}"), b + 1)
                for a in range(2):
                    dve.tensor_reduce(nmax[2 * u + a][:], ps[2 + a][:], AX.X, ALU.max, negate=True)\
                        .then_inc(sem(f"C_max{u}{a}"), 1)

            def copy_pT(b):
                dve.wait_ge(sem("C_ptr11"), b + 1)
                wait(dve, "C_o1", b)
                dve.tensor_copy(probT[3][:], ps[5][:]).then_inc(sem("C_pT11"), 1)

            def sums(b, u):
                dve.wait_ge(sem(f"C_exp{u}0"), b + 1)
                link(dve.tensor_reduce(psums[2 * u][:], prob[2 * u][:], AX.X, ALU.add))

            def normalise(b, u, between=None):
                for a in range(2):
                    if a == 1:
                        if between:
                            between()
                        dve.wait_ge(sem(f"C_exp{u}1"), b + 1)
                    k = 2 * u + a
                    link(dve.reciprocal(psums[k][:], psums[k][:]))
                    dve.tensor_tensor(prob[k][:], prob[k][:], stretch(psums[k][:].unsqueeze(2), 2, P), ALU.mult)\
                        .then_inc(sem(f"C_prob{u}{a}"), 1)

            def copy_k(b, s):
                dve.wait_ge(sem("C_k1"), b + 1)
                wait(dve, "C_s1", b - 1)
                dve.tensor_copy(kT[s][:, GT:2 * GT, :], ps[1][:]).then_inc(sem("C_k1_out"), 1)

            def copy_v(b, s, bank=1):
                dve.wait_ge(sem("C_v1"), b + 1)
                wait(dve, "C_o1", b - 1)
                dve.tensor_copy(v[s][:, 8:16, :], ps[bank][:].rearrange("p t (h d) -> p (t h) d", d=DH)).then_inc(sem("C_v1_out"), 1)

            def add_out(b):
                dve.wait_ge(sem("C_out"), b + 1)
                dve.wait_ge(sem("C_biased"), b + 1)
                xt = xs[:, b:b + 1, :] if isinstance(b, int) else xs[:, bass.ds(b, 1), :]
                dve.tensor_tensor(xt, ps[1][:, 0:1, :], xt, ALU.add).then_inc(sem("C_x"), 1)
                dve.wait_ge(sem("C_x"), b + 1)

            def body(b, s, first=False, last=False):
                peak(b, 0)
                if not first:
                    copy_pT(b - 1)
                sums(b, 0)
                normalise(b, 0)
                if first:
                    copy_v(b + 1, 1 - s, bank=7)
                norm(b, s, c=not isinstance(b, int) or b < B - 2, d=not isinstance(b, int) or b >= 2)
                peak(b, 1)
                if first:
                    copy_k(b + 1, 1 - s)
                else:
                    add_out(b - 1)
                sums(b, 1)
                normalise(b, 1, None if first or last else lambda: copy_k(b + 1, 1 - s))
                if not first and not last:
                    copy_v(b + 1, 1 - s)

            experts(G - 1)
            dve.wait_ge(sem("d_in"), 16 * 4)
            dve.tensor_scalar(gbica[:], gbic[:], LN_ALPHA, None, ALU.add).then_inc(sem("D_bias"), 1)
            link(dve.tensor_scalar(needed[:], iota[:, 0:B], SLOTS + 0.5 / B, -0.5 / B, ALU.mult, ALU.add))
            for b in range(4):
                body(b, b % 2, first=b == 0)
            with dve.Fori(0, B // 2 - 3) as i:
                chain.loop(i, 2 * 8)
                body(2 * i + 4, 0)
                body(2 * i + 5, 1)
            chain.end(B // 2 - 3)
            body(B - 2, 0)
            body(B - 1, 1, last=True)
            def gate_selu(n):
                u, e = chunk_buffer(act_u, n), chunk_buffer(act_e, n)
                dve.wait_ge(sem("D_exp"), n + 1)
                link(dve.tensor_scalar(e, e, SELU_ALPHA, -SELU_ALPHA, ALU.min, ALU.add))
                dve.wait_ge(sem("D_u"), n + 1)
                g, f, _ = gate_chunk(n)
                wait(dve, "D_l", 2 * (g - 1))
                dve.scalar_tensor_tensor(hidD[g % 2][f].rearrange("p (a n) -> p a n", a=F0), u, 0.0, e,
                                         ALU.max, ALU.add).then_inc(sem("D_selu"), 1)

            def gate_top(g, first=0, n=GT):
                dve.wait_ge(sem("D_l"), 2 * g + (first + n) // 2)
                some = slice(first, first + n)
                dve.scalar_tensor_tensor(glog[g % 2][:, some, :], logits_bank(g, first)[:, some, :], SELU_SCALE,
                                         stretch(gbor[:].unsqueeze(1), 1, n), ALU.mult, ALU.add)\
                    .then_inc(sem("D_glog"), 1)
                dve.wait_ge(sem("D_glog"), g + 1 + first // 2)
                tiles = slice(GT * g + first, GT * g + first + n)
                find_top(lambda t: glog[g % 2][:, first + t, :], topD[:, tiles, :], topiD[:, tiles, :], n)

            gate_selu(0)
            copy_pT(B - 1)
            gate_selu(1)
            norm(B, 0, c=False)
            add_out(B - 1)
            gate_selu(2)
            layer_norm([(tile(B - 1, xs), xn[1][:].unsqueeze(1))], "C_ln", 2 * G + B + 3)
            gate_selu(3)
            for g in range(1, G):
                for f in range(F1):
                    gate_selu(F1 * g + f)
                gate_top(g - 1)
            gate_top(G - 1, 0, GT // 2)
            gate_top(G - 1, GT // 2, GT // 2)
            link(dve.tensor_copy(topfD[:], topiD[:, :, 0:2]))
            dve.tensor_scalar(chosen[:], topfD[:], float(E8), None, ALU.is_lt).then_inc(sem("D_chosen"), 1)
            dve.wait_ge(sem("D_chosen"), 1)
            link(dve.tensor_reduce(flag[:], chosen[:], AX.X, ALU.max))

            dve.tensor_reduce(rowsum[:], flag[:], AX.X, ALU.add).then_inc(sem("E_rowsum"), 1)
            link(dve.tensor_tensor_scan(ranks[:], ones[:, 0:B], flag[:], 0.0, ALU.mult, ALU.add))
            link(dve.tensor_tensor(sum16[:].unsqueeze(2), topD[:, :, 0:1], topD[:, :, 1:2], ALU.add))
            link(dve.reciprocal(sum16[:], sum16[:]))
            dve.tensor_tensor(topD[:, :, 0:2], topD[:, :, 0:2], stretch(sum16[:].unsqueeze(2), 2, 2), ALU.mult)\
                .then_inc(sem("D_weights"), 1)
            dve.wait_ge(sem("E_ranked"), 1)
            link(dve.tensor_scalar(ranks[:], ranks[:], ps[5][:, 0, 0:1], None, ALU.add))
            link(dve.tensor_tensor(pos[:], ranks[:], flag[:], ALU.mult))
            link(dve.tensor_scalar(pos[:], pos[:], -1.0, None, ALU.add))
            def make_pick(tiles):
                for t in tiles:
                    last = dve.tensor_scalar(pick[:, t, :], iotab[:], pos[:, t:t + 1], None, ALU.is_equal)
                    if t % GT == GT - 1:
                        last.then_inc(sem("E_pick"), 1)

            dve.tensor_scalar(ranks[:], needed[:], ps[5][:, 1, 0:1], None, ALU.is_lt).then_inc(sem("E_needed"), 1)
            dve.wait_ge(sem("E_needed"), 1)
            link(dve.tensor_reduce(nchf[:], ranks[:], AX.X, ALU.add))
            dve.tensor_copy(nchi[:], nchf[:]).then_inc(sem("E_count"), 1)
            make_pick(range(B))
            eight = stretch(iota[:, 0:E8].unsqueeze(1), 1, B)
            for k in range(2):
                last = dve.tensor_tensor(rt16[:, k, :, :], eight, stretch(topfD[:, :, k:k + 1], 2, E8), ALU.is_equal)
            last.then_inc(sem("D_places"), 1)
            dve.wait_ge(sem("E_count"), 1)
            n_chunks = dve.value_load(nchi[0:1, 0:1], min_val=1, max_val=B // 2)

            def split(parts, value, r):
                link(dve.tensor_copy(parts[0], value))
                link(dve.tensor_tensor(r, value, parts[0], ALU.subtract))
                link(dve.tensor_copy(parts[1], r))
                link(dve.tensor_tensor(r, r, parts[1], ALU.subtract))
                return dve.tensor_copy(parts[2], r)

            with dve.Fori(0, n_chunks) as c:
                chain.loop(c, 5 + 2 * E8 + 4)
                dve.wait_ge(sem("E_gx"), c + 1)
                dve.tensor_copy(xc[:].rearrange("p (h n) -> p h n", h=2), ps[6][:, 0:2, :]).then_inc(sem("E_xc"), 1)
                link(dve.tensor_scalar(pos[:], pos[:], -float(SLOTS), None, ALU.add))
                def selu_half(e, i):
                    dve.wait_ge(sem("E_e"), 2 * (E8 * c + e) + i + 1)
                    ee, u = (buf[e % 2][:, 2 * i:2 * i + 2, :] for buf in (act_e, act_u))
                    link(dve.tensor_scalar(ee, ee, SELU_ALPHA, -SELU_ALPHA, ALU.min, ALU.add))
                    dve.scalar_tensor_tensor(hid[e % 2][:, 2 * i:2 * i + 2, :], u, 0.0, ee, ALU.max, ALU.add)\
                        .then_inc(sem("E_hid"), 1)

                def add(e):
                    dve.wait_ge(sem("E_y"), E8 * c + e + 1)
                    for h in range(2):
                        last = dve.scalar_tensor_tensor(yacc[:, h, :], ps[4 + e % 2][:, h, :], wcs[:, h, e:e + 1],
                                                        yacc[:, h, :], ALU.mult, ALU.add)
                    last.then_inc(sem("E_y_out"), 1)
                    dve.wait_ge(sem("E_y_out"), 2 + E8 * c + e + 1)

                selu_half(0, 0)
                dve.wait_ge(sem("E_gw"), c + 1)
                link(dve.tensor_copy(wc3[:], ps[7][:, 0, 0:2 * 3 * E8].rearrange("p (h k e) -> p h k e", h=2, k=3)))
                link(dve.tensor_tensor(wc[:], wc3[:, :, 0, :], wc3[:, :, 1, :], ALU.add))
                dve.tensor_tensor(wc[:], wc[:], wc3[:, :, 2, :], ALU.add).then_inc(sem("E_wc"), 1)
                dve.wait_ge(sem("E_wc"), c + 1)
                link(dve.tensor_scalar(wcs[:], wc[:], SELU_SCALE, None, ALU.mult))
                selu_half(0, 1)
                dve.wait_ge(sem("E_wtr"), c + 1)
                dve.tensor_copy(wcT[:], ps[7][0:E8, 1:3, :]).then_inc(sem("E_wcT"), 1)
                dve.wait_ge(sem("E_bias"), c + 1)
                link(dve.tensor_copy(yacc[:], ps[7][:, 0:2, :]))
                for e in range(1, E8):
                    selu_half(e, 0)
                    selu_half(e, 1)
                    add(e - 1)
                make_pick(range(0, B // 2))
                add(E8 - 1)
                split([y3[:, k, :, :] for k in range(3)], yacc[:], rest[:].rearrange("p (h n) -> p h n", h=2))\
                    .then_inc(sem("E_y3"), 1)
                make_pick(range(B // 2, B))
                for q in range(G):
                    dve.wait_ge(sem("E_back"), G * c + q + 1)
                    xt = xs[:, GT * q:GT * (q + 1), :]
                    dve.tensor_tensor(xt, ps[6 + q % 2][:], xt, ALU.add).then_inc(sem("E_x"), 1)
            chain.end(0)


_OUT = (B, P, P)


def kernel(**inputs):
    import numpy as np
    import concourse.bacc as bacc
    from concourse.bass_utils import run_bass_kernel_spmd

    a = {k: np.asarray(w) for k, w in inputs.items()}
    laid = {
        "x": a["x"], "ctxT": a["ctx_768"].reshape(B * P, TD).T,
        "Wq0": a["L0_xattn_Wq"], "bq0": a["L0_xattn_bq"], "Wk0": a["L0_xattn_Wk"], "bk0": a["L0_xattn_bk"],
        "Wv0": a["L0_xattn_Wv"], "bv0": a["L0_xattn_bv"], "Wg": a["L0_ffn_Wg"],
        "W1": a["L0_ffn_W1"].transpose(1, 0, 2).reshape(P, -1),
        "W2": a["L0_ffn_W2"].reshape(E8, F0, P, P).transpose(2, 0, 1, 3).reshape(P, -1),
        "Wq1": a["L1_xattn_Wq"], "Wk1": a["L1_xattn_Wk"], "Wv1": a["L1_xattn_Wv"],
        "Wo1": a["L1_xattn_Wo"].reshape(PAIRS, P, P).transpose(1, 0, 2).reshape(P, -1), "bo1": a["L1_xattn_bo"],
        "gwi": a["L1_ffn_gate_wi"], "gbi": a["L1_ffn_gate_bi"].reshape(F1, P).T,
        "gwo": a["L1_ffn_gate_wo"].reshape(F1, P, P).transpose(1, 0, 2).reshape(P, -1), "gbo": a["L1_ffn_gate_bo"],
        "ewi": a["L1_ffn_exp_wi"].transpose(1, 0, 2).reshape(P, -1),
        "ebi": a["L1_ffn_exp_bi"].reshape(E8 * F1, P).T,
        "ewo": a["L1_ffn_exp_wo"].reshape(E8, F1, P, P).transpose(2, 0, 1, 3).reshape(P, -1),
        "ebo": a["L1_ffn_exp_bo"],
    }
    nc = bacc.Bacc("TRN2", target_bir_lowering=False, num_devices=1)
    arrays, args = {}, []
    for name, w in laid.items():
        w = np.ascontiguousarray(w)
        arrays[f"in_{name}"] = w
        args.append(nc.dram_tensor(f"in_{name}", w.shape, mybir.dt.from_np(w.dtype), kind="ExternalInput").ap())
    args.append(nc.dram_tensor("out_x", _OUT, F32, kind="ExternalOutput").ap())
    build(nc, *args)
    result = run_bass_kernel_spmd(nc, [arrays], core_ids=[0])
    return result.results[0]["out_x"]
```
